# Optimizing a Trainium2 kernel written in Bass

```python
import numpy as np
import jax
import jax.numpy as jnp

def _softmax(x, axis=-1):
    return jax.nn.softmax(x, axis=axis)

def _gelu(x):
    return jax.nn.gelu(x, approximate=True)

def _silu(x):
    return jax.nn.silu(x)

def _sigmoid(x):
    return jax.nn.sigmoid(x)

def _layernorm(x, axis=-1, eps=1e-05):
    m = jnp.mean(x, axis=axis, keepdims=True)
    v = jnp.var(x, axis=axis, keepdims=True)
    return (x - m) / jnp.sqrt(v + eps)

def _scatter_add(tgt, idx, src, axis=0):
    return tgt.at[idx].add(src)

def _segment_sum(src, seg, n):
    return jax.ops.segment_sum(src, seg, n)
kernel_name = 'mk_gnn_resnorm_d4_gnn_r8_202e2d'

def setup_inputs(seed: int=0):
    np.random.seed(seed)
    _w = jnp.asarray

    def _rec_inputs():
        import jax
        import jax.numpy as jnp
        _gk = jax.random.key(seed)
        x = -0.001003 + 1 * jax.random.normal(jax.random.fold_in(_gk, 1), (256, 768), jnp.float32)
        src = jax.random.randint(jax.random.fold_in(_gk, 2), (4096,), 0, 256, jnp.int32)
        dst = jnp.minimum((256 * jax.random.uniform(jax.random.fold_in(_gk, 3), (4096,)) ** 2.0).astype(jnp.int32), 2047)
        _o = jnp.argsort(dst, stable=True)
        src = src[_o]
        dst = dst[_o]
        edge_type_3 = jax.random.randint(jax.random.fold_in(_gk, 12), (4096,), 0, 3, jnp.int32)
        return (x, src, dst, edge_type_3)
    x, src, dst, edge_type_3 = _rec_inputs()

    def _L0_gnn_setup():
        import jax, jax.numpy as jnp
        import numpy as np
        NUM_RELATIONS = 3

        def _rgcn(x, W_rel, W_root, bias, src, dst, etype):
            n = x.shape[0]
            xr = jnp.einsum('ni,rio->rno', x, W_rel)
            msg = xr[etype, src]
            out = x @ W_root + bias
            for r in range(NUM_RELATIONS):
                m = etype == r
                s = jax.ops.segment_sum(jnp.where(m[:, None], msg, 0.0), dst, num_segments=n)
                c = jax.ops.segment_sum(m.astype(x.dtype), dst, num_segments=n)
                out = out + s / jnp.maximum(c, 1.0)[:, None]
            return out

        def _gate(h, q, Wg, bg, Wq, bq):
            B, L, F = q.shape
            N = h.shape[0] // B
            h3 = h.reshape(B, N, F)
            hg = jnp.einsum('bnf,gf->bng', h3, Wg[:, :F])
            qg = jnp.einsum('blf,gf->blg', q, Wg[:, F:]) + bg
            attn = jax.nn.sigmoid(hg[:, :, None, :] + qg[:, None, :, :])
            qi = jnp.einsum('bnlf,blf->bnf', attn, q)
            alpha = jax.nn.sigmoid(jnp.einsum('bnf,gf->bng', h3, Wq[:, :F]) + jnp.einsum('bnf,gf->bng', qi, Wq[:, F:]) + bq)
            hn = alpha * jnp.tanh(qi) + (1.0 - alpha) * h3
            return hn.reshape(B * N, F)
        key = jax.random.key(seed)
        ks = jax.random.split(key, 16)
        F = 768
        BN, E, B, L = (256, 8192, 8, 64)
        s = 0.02
        return {'x': jax.random.normal(ks[0], (BN, F), jnp.float32), 'edge_index': jax.random.randint(ks[1], (2, E), 0, BN), 'edge_type': jax.random.randint(ks[2], (E,), 0, NUM_RELATIONS), 'query_embs': jax.random.normal(ks[3], (B, L, F), jnp.float32), 'W_rel1': jax.random.normal(ks[4], (NUM_RELATIONS, F, F), jnp.float32) * s, 'W_root1': jax.random.normal(ks[5], (F, F), jnp.float32) * s, 'b1': jnp.zeros((F,), jnp.float32), 'W_rel2': jax.random.normal(ks[6], (NUM_RELATIONS, F, F), jnp.float32) * s, 'W_root2': jax.random.normal(ks[7], (F, F), jnp.float32) * s, 'b2': jnp.zeros((F,), jnp.float32), 'Wg': jax.random.normal(ks[8], (F, 2 * F), jnp.float32) * s, 'bg': jnp.zeros((F,), jnp.float32), 'Wq': jax.random.normal(ks[9], (F, 2 * F), jnp.float32) * s, 'bq': jnp.zeros((F,), jnp.float32)}
    _L0_gnn_all = _L0_gnn_setup()
    _L0_gnn_in = {k: v for k, v in _L0_gnn_all.items() if k in ('query_embs', 'W_rel1', 'W_root1', 'b1', 'W_rel2', 'W_root2', 'b2', 'Wg', 'bg', 'Wq', 'bq')}
    del _L0_gnn_all

    def _L1_gnn_setup():
        import jax, jax.numpy as jnp
        import numpy as np
        N_NODES = 1250
        D = 768
        N_EDGES = 20000

        def gcn_conv(x, W, b, src, dst, n_nodes):
            h = x @ W
            deg = jax.ops.segment_sum(jnp.ones_like(dst, dtype=h.dtype), dst, num_segments=n_nodes)
            dinv = jnp.where(deg > 0, jax.lax.rsqrt(deg), 0.0)
            norm = dinv[src] * dinv[dst]
            msgs = h[src] * norm[:, None]
            out = jax.ops.segment_sum(msgs, dst, num_segments=n_nodes)
            return out + b

        def add_self_loops(edge_index, n_nodes):
            loop = jnp.arange(n_nodes, dtype=edge_index.dtype)
            src = jnp.concatenate([edge_index[0], loop])
            dst = jnp.concatenate([edge_index[1], loop])
            return (src, dst)
        key = jax.random.key(seed)
        k1, k2, k3, k4 = jax.random.split(key, 4)
        x = jax.random.normal(k1, (N_NODES, D), dtype=jnp.float32)
        edge_index = jax.random.randint(k2, (2, N_EDGES), 0, N_NODES, dtype=jnp.int32)
        glorot = float(np.sqrt(6.0 / (D + D)))
        W1 = jax.random.uniform(k3, (D, D), jnp.float32, -glorot, glorot)
        W2 = jax.random.uniform(k4, (D, D), jnp.float32, -glorot, glorot)
        b1 = jnp.zeros((D,), jnp.float32)
        b2 = jnp.zeros((D,), jnp.float32)
        return {'x': x, 'W1': W1, 'b1': b1, 'W2': W2, 'b2': b2, 'edge_index': edge_index}
    _L1_gnn_all = _L1_gnn_setup()
    _L1_gnn_in = {k: v for k, v in _L1_gnn_all.items() if k in ('W1', 'b1', 'W2', 'b2')}
    del _L1_gnn_all

    def _L2_gnn_setup():
        import jax, jax.numpy as jnp
        import numpy as np
        N_NODES = 1250
        N_EDGES = 12500
        DIM = 768
        key = jax.random.key(seed)
        k1, k2, k3, k4 = jax.random.split(key, 4)
        x = jax.random.normal(k1, (N_NODES, DIM), dtype=jnp.float32)
        edge_index = jax.random.randint(k2, (2, N_EDGES), 0, N_NODES, dtype=jnp.int32)
        W = jax.random.normal(k3, (DIM, DIM), dtype=jnp.float32) / np.sqrt(DIM)
        b = jnp.zeros((DIM,), dtype=jnp.float32)
        return {'x': x, 'edge_index': edge_index, 'W': W, 'b': b}
    _L2_gnn_all = _L2_gnn_setup()
    _L2_gnn_in = {k: v for k, v in _L2_gnn_all.items() if k in ('W', 'b')}
    del _L2_gnn_all

    def _L3_gnn_setup():
        import jax, jax.numpy as jnp
        import numpy as np
        NEG_SLOPE = 0.2
        EPS = 1e-16
        N_NODES = 4096
        N_EDGES = 20000
        DIM = 768
        HEADS1 = 4
        OUT1 = DIM // HEADS1
        HEADS2 = 1
        OUT2 = DIM
        N_REL = 3

        def rgat_conv(x, W, q, k, b, src, dst, etype, heads, out_ch, n_nodes):
            xr = jnp.einsum('nd,rdf->rnf', x, W)
            oi = xr[etype, dst]
            oj = xr[etype, src]
            qi = oi @ q
            kj = oj @ k
            alpha = jax.nn.leaky_relu(qi + kj, NEG_SLOPE)
            m = jax.ops.segment_max(alpha, dst, num_segments=n_nodes)
            e = jnp.exp(alpha - m[dst])
            z = jax.ops.segment_sum(e, dst, num_segments=n_nodes)
            a = e / (z[dst] + EPS)
            msg = (a[:, :, None] * oj.reshape(-1, heads, out_ch)).reshape(-1, heads * out_ch)
            out = jax.ops.segment_sum(msg, dst, num_segments=n_nodes)
            return out + b
        key = jax.random.key(seed)
        ks = jax.random.split(key, 12)
        s = 0.02
        return {'x': jax.random.normal(ks[0], (N_NODES, DIM), dtype=jnp.float32), 'edge_index': jax.random.randint(ks[1], (2, N_EDGES), 0, N_NODES, dtype=jnp.int64), 'edge_type': jax.random.randint(ks[2], (N_EDGES,), 0, N_REL, dtype=jnp.int64), 'W1': jax.random.normal(ks[3], (N_REL, DIM, HEADS1 * OUT1), dtype=jnp.float32) * s, 'q1': jax.random.normal(ks[4], (HEADS1 * OUT1, HEADS1), dtype=jnp.float32) * s, 'k1': jax.random.normal(ks[5], (HEADS1 * OUT1, HEADS1), dtype=jnp.float32) * s, 'b1': jnp.zeros((HEADS1 * OUT1,), dtype=jnp.float32), 'W2': jax.random.normal(ks[6], (N_REL, DIM, HEADS2 * OUT2), dtype=jnp.float32) * s, 'q2': jax.random.normal(ks[7], (HEADS2 * OUT2, HEADS2), dtype=jnp.float32) * s, 'k2': jax.random.normal(ks[8], (HEADS2 * OUT2, HEADS2), dtype=jnp.float32) * s, 'b2': jnp.zeros((HEADS2 * OUT2,), dtype=jnp.float32)}
    _L3_gnn_all = _L3_gnn_setup()
    _L3_gnn_in = {k: v for k, v in _L3_gnn_all.items() if k in ('W1', 'q1', 'k1', 'b1', 'W2', 'q2', 'k2', 'b2')}
    del _L3_gnn_all
    return {'x': x, 'src': src, 'dst': dst, 'edge_type_3': edge_type_3, 'L0_gnn_query_embs': _L0_gnn_in['query_embs'], 'L0_gnn_W_rel1': _L0_gnn_in['W_rel1'], 'L0_gnn_W_root1': _L0_gnn_in['W_root1'], 'L0_gnn_b1': _L0_gnn_in['b1'], 'L0_gnn_W_rel2': _L0_gnn_in['W_rel2'], 'L0_gnn_W_root2': _L0_gnn_in['W_root2'], 'L0_gnn_b2': _L0_gnn_in['b2'], 'L0_gnn_Wg': _L0_gnn_in['Wg'], 'L0_gnn_bg': _L0_gnn_in['bg'], 'L0_gnn_Wq': _L0_gnn_in['Wq'], 'L0_gnn_bq': _L0_gnn_in['bq'], 'L1_gnn_W1': _L1_gnn_in['W1'], 'L1_gnn_b1': _L1_gnn_in['b1'], 'L1_gnn_W2': _L1_gnn_in['W2'], 'L1_gnn_b2': _L1_gnn_in['b2'], 'L2_gnn_W': _L2_gnn_in['W'], 'L2_gnn_b': _L2_gnn_in['b'], 'L3_gnn_W1': _L3_gnn_in['W1'], 'L3_gnn_q1': _L3_gnn_in['q1'], 'L3_gnn_k1': _L3_gnn_in['k1'], 'L3_gnn_b1': _L3_gnn_in['b1'], 'L3_gnn_W2': _L3_gnn_in['W2'], 'L3_gnn_q2': _L3_gnn_in['q2'], 'L3_gnn_k2': _L3_gnn_in['k2'], 'L3_gnn_b2': _L3_gnn_in['b2']}

def reference(x, src, dst, edge_type_3, L0_gnn_query_embs, L0_gnn_W_rel1, L0_gnn_W_root1, L0_gnn_b1, L0_gnn_W_rel2, L0_gnn_W_root2, L0_gnn_b2, L0_gnn_Wg, L0_gnn_bg, L0_gnn_Wq, L0_gnn_bq, L1_gnn_W1, L1_gnn_b1, L1_gnn_W2, L1_gnn_b2, L2_gnn_W, L2_gnn_b, L3_gnn_W1, L3_gnn_q1, L3_gnn_k1, L3_gnn_b1, L3_gnn_W2, L3_gnn_q2, L3_gnn_k2, L3_gnn_b2):
    import jax
    import jax.numpy as jnp

    def _L0_gnn_ref(x, edge_index, edge_type, query_embs, W_rel1, W_root1, b1, W_rel2, W_root2, b2, Wg, bg, Wq, bq):
        import jax, jax.numpy as jnp
        import numpy as np
        NUM_RELATIONS = 3

        def _rgcn(x, W_rel, W_root, bias, src, dst, etype):
            n = x.shape[0]
            xr = jnp.einsum('ni,rio->rno', x, W_rel)
            msg = xr[etype, src]
            out = x @ W_root + bias
            for r in range(NUM_RELATIONS):
                m = etype == r
                s = jax.ops.segment_sum(jnp.where(m[:, None], msg, 0.0), dst, num_segments=n)
                c = jax.ops.segment_sum(m.astype(x.dtype), dst, num_segments=n)
                out = out + s / jnp.maximum(c, 1.0)[:, None]
            return out

        def _gate(h, q, Wg, bg, Wq, bq):
            B, L, F = q.shape
            N = h.shape[0] // B
            h3 = h.reshape(B, N, F)
            hg = jnp.einsum('bnf,gf->bng', h3, Wg[:, :F])
            qg = jnp.einsum('blf,gf->blg', q, Wg[:, F:]) + bg
            attn = jax.nn.sigmoid(hg[:, :, None, :] + qg[:, None, :, :])
            qi = jnp.einsum('bnlf,blf->bnf', attn, q)
            alpha = jax.nn.sigmoid(jnp.einsum('bnf,gf->bng', h3, Wq[:, :F]) + jnp.einsum('bnf,gf->bng', qi, Wq[:, F:]) + bq)
            hn = alpha * jnp.tanh(qi) + (1.0 - alpha) * h3
            return hn.reshape(B * N, F)
        src, dst = (edge_index[0], edge_index[1])
        h = jax.nn.relu(_rgcn(x, W_rel1, W_root1, b1, src, dst, edge_type))
        h = _gate(h, query_embs, Wg, bg, Wq, bq)
        h = jax.nn.relu(_rgcn(h, W_rel2, W_root2, b2, src, dst, edge_type))
        h = _gate(h, query_embs, Wg, bg, Wq, bq)
        return h

    def _L1_gnn_ref(x, W1, b1, W2, b2, edge_index):
        import jax, jax.numpy as jnp
        import numpy as np
        N_NODES = 1250
        D = 768
        N_EDGES = 20000

        def gcn_conv(x, W, b, src, dst, n_nodes):
            h = x @ W
            deg = jax.ops.segment_sum(jnp.ones_like(dst, dtype=h.dtype), dst, num_segments=n_nodes)
            dinv = jnp.where(deg > 0, jax.lax.rsqrt(deg), 0.0)
            norm = dinv[src] * dinv[dst]
            msgs = h[src] * norm[:, None]
            out = jax.ops.segment_sum(msgs, dst, num_segments=n_nodes)
            return out + b

        def add_self_loops(edge_index, n_nodes):
            loop = jnp.arange(n_nodes, dtype=edge_index.dtype)
            src = jnp.concatenate([edge_index[0], loop])
            dst = jnp.concatenate([edge_index[1], loop])
            return (src, dst)
        n = x.shape[0]
        src, dst = add_self_loops(edge_index, n)
        h = gcn_conv(x, W1, b1, src, dst, n)
        h = jax.nn.relu(h)
        out = gcn_conv(h, W2, b2, src, dst, n)
        return out

    def _L2_gnn_ref(x, edge_index, W, b):
        import jax, jax.numpy as jnp
        import numpy as np
        N_NODES = 1250
        N_EDGES = 12500
        DIM = 768
        n = x.shape[0]
        loop = jnp.arange(n, dtype=edge_index.dtype)
        src = jnp.concatenate([edge_index[0], loop])
        dst = jnp.concatenate([edge_index[1], loop])
        deg = jax.ops.segment_sum(jnp.ones_like(dst, dtype=x.dtype), dst, num_segments=n)
        deg_inv_sqrt = jnp.where(deg > 0, jax.lax.rsqrt(deg), 0.0)
        norm = deg_inv_sqrt[src] * deg_inv_sqrt[dst]
        h = x @ W
        msg = h[src] * norm[:, None]
        out = jax.ops.segment_sum(msg, dst, num_segments=n)
        return out + b

    def _L3_gnn_ref(x, edge_index, edge_type, W1, q1, k1, b1, W2, q2, k2, b2):
        import jax, jax.numpy as jnp
        import numpy as np
        NEG_SLOPE = 0.2
        EPS = 1e-16
        N_NODES = 4096
        N_EDGES = 20000
        DIM = 768
        HEADS1 = 4
        OUT1 = DIM // HEADS1
        HEADS2 = 1
        OUT2 = DIM
        N_REL = 3

        def rgat_conv(x, W, q, k, b, src, dst, etype, heads, out_ch, n_nodes):
            xr = jnp.einsum('nd,rdf->rnf', x, W)
            oi = xr[etype, dst]
            oj = xr[etype, src]
            qi = oi @ q
            kj = oj @ k
            alpha = jax.nn.leaky_relu(qi + kj, NEG_SLOPE)
            m = jax.ops.segment_max(alpha, dst, num_segments=n_nodes)
            e = jnp.exp(alpha - m[dst])
            z = jax.ops.segment_sum(e, dst, num_segments=n_nodes)
            a = e / (z[dst] + EPS)
            msg = (a[:, :, None] * oj.reshape(-1, heads, out_ch)).reshape(-1, heads * out_ch)
            out = jax.ops.segment_sum(msg, dst, num_segments=n_nodes)
            return out + b
        src, dst = (edge_index[0], edge_index[1])
        n = x.shape[0]
        h = rgat_conv(x, W1, q1, k1, b1, src, dst, edge_type, HEADS1, OUT1, n)
        h = jax.nn.elu(h)
        out = rgat_conv(h, W2, q2, k2, b2, src, dst, edge_type, HEADS2, OUT2, n)
        return out
    edge_index = jnp.stack([src, dst])
    x = _layernorm(x + _L0_gnn_ref(x, edge_index, edge_type_3, L0_gnn_query_embs, L0_gnn_W_rel1, L0_gnn_W_root1, L0_gnn_b1, L0_gnn_W_rel2, L0_gnn_W_root2, L0_gnn_b2, L0_gnn_Wg, L0_gnn_bg, L0_gnn_Wq, L0_gnn_bq), axis=-1)
    x = _layernorm(x + _L1_gnn_ref(x, L1_gnn_W1, L1_gnn_b1, L1_gnn_W2, L1_gnn_b2, edge_index), axis=-1)
    x = _layernorm(x + _L2_gnn_ref(x, edge_index, L2_gnn_W, L2_gnn_b), axis=-1)
    x = _layernorm(x + _L3_gnn_ref(x, edge_index, edge_type_3, L3_gnn_W1, L3_gnn_q1, L3_gnn_k1, L3_gnn_b1, L3_gnn_W2, L3_gnn_q2, L3_gnn_k2, L3_gnn_b2), axis=-1)
    return x

_drawn_inputs = setup_inputs


def setup_inputs(seed=0):
    import zlib

    import numpy as np

    out = dict(_drawn_inputs(seed))
    spreads = {'L0_gnn_b1': (0.0, 0.516),
     'L0_gnn_b2': (0.0, 0.1),
     'L0_gnn_bg': (0.0, 0.441),
     'L0_gnn_bq': (0.0, 0.53),
     'L1_gnn_b1': (0.0, 0.1),
     'L1_gnn_b2': (0.0, 0.1),
     'L2_gnn_b': (0.0, 0.1),
     'L3_gnn_b1': (0.0, 0.1),
     'L3_gnn_b2': (0.0, 0.1)}
    factors = {'L3_gnn_q1': 8.0, 'L3_gnn_k1': 8.0, 'L3_gnn_q2': 8.0, 'L3_gnn_k2': 8.0}
    for name, (base, spread) in spreads.items():
        noise = np.random.default_rng([zlib.crc32(name.encode()), seed]).standard_normal(out[name].shape)
        drawn = base * np.exp(spread * noise) if base else spread * noise
        out[name] = jnp.asarray(drawn.astype(out[name].dtype))
    for name, factor in factors.items():
        out[name] = (out[name] * factor).astype(out[name].dtype)
    return out
```

```python
from contextlib import ExitStack

import concourse.bass as bass
from concourse import mybir

P = 128
N = 256
NM = N // P
F = 768
FC = F // P
FH = F // 2
E = 4096
EC = E // P
R = 3
B = 8
NB = N // B
L = 64
LH = 32
NJ = 4
JS = NB // NJ
STEPS = B * JS
HEADS = (4, 1)
BANKS = 8
RING_PRE = 3
RING_POST = 5
HOT = 4
ATT = 4
BIG = 1e30
EPS = 1e-5
EPS_Z = 1e-16
SLOPE = 0.2

ALU = mybir.AluOpType
ACT = mybir.ActivationFunctionType
AX = mybir.AxisListType
F32 = mybir.dt.float32
F32R = mybir.dt.float32r
F16 = mybir.dt.float16
BF16 = mybir.dt.bfloat16
I32 = mybir.dt.int32

WEIGHTS = (["WgT_q"] + [f"Wrel1_{r}" for r in range(R)] + ["Wroot1", "WgT_h", "WqT_h", "WqT_q"]
           + [f"Wrel2_{r}" for r in range(R)] + ["Wroot2", "WgT_h", "WqT_h", "WqT_q"]
           + ["gcn1", "gcn2"] + [f"W1T_{r}" for r in range(R)] + ["gcn3"] + [f"W2T_{r}" for r in range(R)]
           + [f"W1_{r}" for r in range(R)] + [f"W2_{r}" for r in range(R)])
PRE = 15


def weight_slot(i):
    return i % RING_PRE if i < PRE else (i - PRE) % RING_POST


def weight_before(i):
    for k in range(i - 1, -1, -1):
        if weight_slot(k) == weight_slot(i):
            return k
    return None


def weight_uses(i):
    return sum(weight_slot(k) == weight_slot(i) for k in range(i + 1))


def plan_tiles():
    t = [(("A", m, h), "AV"[h]) for m in range(NM) for h in range(2)]
    t += [(("qg", c, h), "V") for c in range(4) for h in range(2)]
    for g in range(2):
        if g == 0:
            t += [(("AnT", s, r), "AV"[r % 2]) for s in range(NM) for r in range(R)]
            t += [(("AgT", s), "V") for s in range(NM)]
        t += [(("Y", g, r, m, h), "AV"[h]) for r in range(R) for m in range(NM) for h in range(2)]
        t += [(("agg", g, c), "AV"[c % 2]) for c in range(FC)]
        t += [(("hg", g, m, h), "V") for m in range(NM) for h in range(2)]
        t += [(("alpha", g, c), "A") for c in range(FC)]
    t += [(("back", m, h), "V") for m in range(NM) for h in range(2)]
    t += [(("xT", 0, c), "AV"[c % 2]) for c in range(FC)]
    t += [(("Yg", 0, m, h), "AV"[h]) for m in range(NM) for h in range(2)]
    t += [(("agg", 2, c), "AV"[c % 2]) for c in range(FC)]
    t += [(("Yg", 1, m, h), "AV"[h]) for m in range(NM) for h in range(2)]
    t += [(("out", 0, m, h), "V") for m in range(NM) for h in range(2)]
    t += [(("wqk", 0), "A")]
    t += [(("xT", 1, c), "AV"[c % 2]) for c in range(FC)]
    t += [(("Yg", 2, m, h), "AV"[h]) for m in range(NM) for h in range(2)]
    t += [(("out", 1, m, h), "V") for m in range(NM) for h in range(2)]
    t += [(("wqk", 1), "A")]
    t += [(("xT", 2, c), "AV"[c % 2]) for c in range(FC)]
    for k in range(2):
        t += [(("QN", k), "A"), (("KT", k), "A")]
        t += [(("Kb", k, i), "A") for i in range((HEADS[k] * R + 1) // 2)]
        t += [(("Yr", k, r, m, h), "A") for r in range(R) for m in range(NM) for h in range(2)]
        t += [(("PT", k, m, h, s), "AV"[s]) for m in range(NM) for h in range(HEADS[k]) for s in range(NM)]
        if k == 0:
            t += [(("att", m, h), "V") for m in range(NM) for h in range(2)]
            t += [(("hT", c), "A") for c in range(FC)]
        else:
            t += [(("out", 2, m, h), "V") for m in range(NM) for h in range(2)]
    return t


TILES = plan_tiles()
NUMBER = {name: i for i, (name, _) in enumerate(TILES)}
DRAINS = {name: sum(e == TILES[i][1] for _, e in TILES[:i + 1]) for name, i in NUMBER.items()}


def build(nc, a, out):
    ctx = ExitStack()
    with ctx:
        def sem(name):
            return ctx.enter_context(nc.semaphore(name))

        def sb(name, shape, dt=F32, stack=ctx):
            return stack.enter_context(nc.sbuf_tensor(name, shape, dt))

        W = sb("weight_slots", [P, RING_PRE, FC, F])
        HA = sb("colsA", [P, FC, N])
        HB = sb("colsB", [P, FC, N])
        XT = sb("x_cols", [P, FC, N])
        QX = sb("qi_cols_or_x_rows", [P, NM * F])
        TY = sb("tanh_cols_or_y_rows", [P, NM * F])
        Y = sb("products", [P, NM, R, F])
        Acnt = sb("edge_counts", [P, NM, R, N])
        AnT = sb("mean_weights_T", [P, NM, R, N])
        AgT = sb("gcn_weights_T", [P, NM, N])
        ident = sb("ident", [P, P])
        sel = sb("gate_select", [P, JS, P], F32R)
        ones4 = sb("ones_per_node", [P, NJ])
        bcol = sb("bias_cols", [P, 5, FC])
        qk = [sb(f"qk{k}", [P, FC, 2 * HEADS[k]]) for k in range(2)]
        wqk = [sb(f"wqk{k}", [P, FC, R * 2 * HEADS[k]]) for k in range(2)]
        QN = sb("q_of_node", [P, NM, R * 2 * HEADS[0]])
        KT = sb("k_rows", [R * 2 * HEADS[0], N])
        idxf = sb("edge_floats", [P, 3, EC])
        comb = sb("edge_rel_src", [P, EC])
        cnt = sb("counts", [P, NM, 8])
        stat = sb("bn_stats", [P, NM, 2, 6])
        mv = sb("mean_var", [P, NM, 4])
        smx = sb("softmax_small", [P, NM, 4, HEADS[0]])
        epsc = sb("eps", [P, 1])

        early, late = ExitStack(), ExitStack()
        Mt = sb("gate_moving", [P, B, 2, F], F32R, early)
        qrep = sb("q_replicated", [P, 2, 2, F], F32, early)
        att = sb("gate_attention", [P, ATT, 2, F], F32, early)
        early.close()
        Wx = sb("weight_slots_late", [P, RING_POST - RING_PRE, FC, F], F32, late)
        U = sb("edge_scores", [P, NM, HEADS[0], R, N], F32, late)
        PT = sb("edge_weights_T", [P, NM, HEADS[0], R, N], F32, late)
        late.close()

        def flat(t):
            return t[:, :, :].rearrange("p c n -> p (c n)")

        hot = [Y[:, 0, :, :].rearrange("p r f -> p (r f)").bitcast(BF16)[:, 1024 * i:1024 * (i + 1)]
               for i in range(HOT)]
        iota_i = flat(HA)[:, 0:F].bitcast(I32)
        iota_h = flat(HB)[:, 0:F // 2].bitcast(F16)
        spare = AnT[:, :, :, :].rearrange("p m r n -> p (m r n)")
        bg_row, ones_row = spare[0:1, 0:F], spare[0:1, F:F + P]
        idx = spare[:, F + P:F + P + 3 * EC].bitcast(I32).rearrange("p (k c) -> p k c", k=3)
        qT = [t[:, :].rearrange("p (c l) -> p c l", c=FC // 2) for t in (QX, TY)]
        qg_hi = att[:, 0:2, :, :].rearrange("p a h f -> p (a h) f")
        qg_lo = att[:, 2:4, :, :].rearrange("p a h f -> p (a h) f")
        AnS = flat(HA).rearrange("p (m r n) -> p m r n", m=NM, r=R)
        AgS = flat(HB)[:, F:F + NM * N].rearrange("p (m n) -> p m n", m=NM)
        hg_hi = [Y[:, 0, m, :] for m in range(NM)]
        hg_lo = [Y[:, 1, m, :] for m in range(NM)]
        qiT = QX[:, :].rearrange("p (c n) -> p c n", c=FC)
        thT = TY[:, :].rearrange("p (c n) -> p c n", c=FC)
        alpha = att[:, 0, :, :].rearrange("p h f -> p (h f)").rearrange("p (c n) -> p c n", c=FC)
        xrows = QX[:, :].rearrange("p (m f) -> p m f", m=NM)
        yrows = TY[:, :].rearrange("p (m f) -> p m f", m=NM)
        brow = flat(XT).rearrange("p (m f) -> p m f", m=NM)
        xplus = [[Y[:, m, 2, :] for m in range(NM)]] * 2 + [
            [flat(HB)[:, m * F:(m + 1) * F] for m in range(NM)]]
        hide = AnT
        elu_m = U[:, 0, 0:2, :, :].rearrange("p h r n -> p (h r n)")
        Mt_graph = Mt[:, :, :, :].rearrange("p b h f -> p b (h f)")

        ps = ctx.enter_context(nc.psum_tensor("ps", [P, BANKS, 512], F32))
        gsum = [ps[:, 3 * i:3 * i + 3, :].rearrange("p b n -> p (b n)") for i in range(2)]
        gqi = [ps[:, 6 + i, 0:FC * NB].rearrange("p (c n) -> p c n", c=FC) for i in range(2)]

        def wslot(i):
            s = weight_slot(i)
            return W[:, s, :, :] if s < RING_PRE else Wx[:, s - RING_PRE, :, :]

        def psum(name, width, parts=P):
            return ps[0:parts, NUMBER[name] % BANKS, 0:width]

        tile_full = sem("tile_full")
        drained = {"A": sem("drained_by_act"), "V": sem("drained_by_dve")}
        weight_in = [sem(f"weight_in{s}") for s in range(RING_POST)]
        weights_used = sem("weights_used")
        ints_in = sem("ints_in")
        x_in = sem("x_in")
        q_in = sem("q_in")
        small_in = sem("small_in")
        const_made = sem("const_made")
        iota_made = sem("iota_made")
        sel_made = sem("sel_made")
        hot_ready = sem("hot_ready")
        hot_used = sem("hot_used")
        deg_ready = sem("deg_ready")
        root_ready = sem("root_ready")
        graph_ready = sem("graph_ready")
        qg_hi_ready = sem("qg_hi_ready")
        qg_placed = sem("qg_placed")
        hg_hi_ready = sem("hg_hi_ready")
        hg_in = [sem(f"hg_in{b}") for b in range(B)]
        hg_placed = sem("hg_placed")
        qrep_in = [sem(f"qrep_in{u}") for u in range(2)]
        sum_ready = sem("sum_ready")
        sig_ready = sem("sig_ready")
        prod_ready = sem("prod_ready")
        prods_summed = sem("prods_summed")
        qi_copied = sem("qi_copied")
        tanh_ready = sem("tanh_ready")
        h_out = sem("h_out")
        dve_chain = sem("dve_chain")
        var_ready = sem("var_ready")
        std_ready = sem("std_ready")
        x_ready = sem("x_ready")
        brow_in = sem("brow_in")
        xplus_ready = sem("xplus_ready")
        u_ready = sem("u_ready")
        nmax_ready = sem("nmax_ready")
        e_ready = sem("e_ready")
        p_ready = sem("p_ready")
        elu_min = sem("elu_min")
        elu_exp = sem("elu_exp")
        out_done = sem("out_done")

        block = ctx.enter_context(nc.Block())

        def wait_drained(eng, *names):
            most = {}
            for name in names:
                e = TILES[NUMBER[name]][1]
                most[e] = max(most.get(e, 0), DRAINS[name])
            for e, n in most.items():
                eng.wait_ge(drained[e], n)

        def wait_full(eng, name):
            eng.wait_ge(tile_full, NUMBER[name] + 1)

        @block.sync
        def _(sp):
            for k, name in enumerate(("dst", "src", "etype")):
                sp.dma_start(idx[:, k, :], a[name].rearrange("(p c) -> p c", p=P)).then_inc(ints_in, 16)

            def load(i):
                before = weight_before(i)
                if before is not None:
                    sp.wait_ge(weights_used, before + 1)
                sp.dma_start(wslot(i), a[WEIGHTS[i]].rearrange("(c p) n -> p c n", p=P)).then_inc(
                    weight_in[weight_slot(i)], 16)

            qT_rows = a["qT"].rearrange("(c p) n -> p c n", p=P)
            for k in range(2):
                sp.dma_start(qT[k], qT_rows[:, 3 * k:3 * k + 3, :]).then_inc(q_in, 16)
            sp.dma_start(bg_row[:, :], a["bg"]).then_inc(small_in, 16)
            load(0)
            sp.dma_start(XT[:, :, :], a["xT"].rearrange("(c p) n -> p c n", p=P)).then_inc(x_in, 16)
            load(1)
            sp.dma_start(bcol[:, :, :], a["bias_cols"]).then_inc(small_in, 16)
            for k in range(2):
                sp.dma_start(qk[k][:, :, :], a[f"qk{k}"]).then_inc(small_in, 16)

            q_rows = a["q"].rearrange("(b h l) f -> b l h f", h=2, l=LH)

            def place_q(g, b, u):
                for n in range(NJ):
                    sp.dma_start(qrep[n * LH:(n + 1) * LH, u, :, :],
                                 q_rows[bass.ds(b, 1), :, :, :].rearrange("o l h f -> (o l) h f")).then_inc(
                        qrep_in[u], 16)

            for i in range(2, 9):
                load(i)
            for g in range(2):
                if g == 1:
                    for i in range(9, PRE + 1):
                        load(i)
                for u in range(2):
                    if g == 1:
                        sp.wait_ge(prod_ready, STEPS + JS * (u - 1))
                    place_q(g, u, u)
                with sp.Fori(1, B // 2) as i2:
                    for u in range(2):
                        sp.wait_ge(prod_ready, i2 * (2 * JS) + (STEPS * g + JS * (u - 1)))
                        place_q(g, i2 * 2 + u, u)
            for i in range(PRE + 1, len(WEIGHTS)):
                if i == PRE + RING_PRE:
                    sp.wait_ge(h_out, 2 * FC + 1)
                    for k in range(2):
                        sp.dma_start(brow[:, k, :], a[f"brow{k}"].partition_broadcast(P)).then_inc(brow_in, 16)
                load(i)
                if WEIGHTS[i] == "W2T_2":
                    sp.wait_ge(xplus_ready, 1)
                    sp.dma_start(brow[:, 0, :], a["brow2"].partition_broadcast(P)).then_inc(brow_in, 16)
            for m in range(NM):
                sp.wait_ge(x_ready, NM * 3 + m + 1)
                sp.dma_start(out[m * P:(m + 1) * P, :], xrows[:, m, :]).then_inc(out_done, 16)
            sp.wait_ge(out_done, 16 * NM)

        @block.gpsimd
        def _(pool):
            pool.iota(iota_i, [[1, F]], base=0, channel_multiplier=0).then_inc(iota_made, 1)
            pool.memset(ident[:, :], 0.0).then_inc(const_made, 1)
            pool.memset(ones4[:, :], 0.0).then_inc(const_made, 1)
            pool.wait_ge(const_made, 2)
            pool.affine_select(out=ident[:, :], in_=ident[:, :], compare_op=ALU.not_equal, fill=1.0, base=0,
                               pattern=[[-1, P]], channel_multiplier=1).then_inc(const_made, 1)
            for n in range(NJ):
                pool.wait_ge(const_made, 3 + n)
                pool.memset(ones4[n * LH:(n + 1) * LH, n:n + 1], 1.0).then_inc(const_made, 1)
            pool.wait_ge(const_made, 7)
            pool.memset(ones_row[:, :], 1.0).then_inc(const_made, 1)
            pool.wait_ge(const_made, 8)
            pool.memset(epsc[:, :], EPS).then_inc(const_made, 1)
            wait_drained(pool, ("qg", 3, 1))
            for part, rows in ((0, qg_hi), (1, qg_lo)):
                for b2 in range(2):
                    for h in range(2):
                        p0 = (2 * b2 + h) * LH
                        dst = Mt[part * LH:(part + 1) * LH, b2:B:2, h, :].bitcast(F32)
                        pool.dma_start(dst, rows[p0:p0 + LH, :, :]).then_inc(qg_placed, 16)
            pool.wait_ge(qg_placed, 16 * 8)
            pool.sem_inc(prods_summed, ATT)
            for g in range(2):
                for m in range(NM):
                    wait_drained(pool, ("hg", g, m, 1))
                    for q in range(B // NM):
                        b = m * (B // NM) + q
                        for part, rows in ((2, hg_hi), (3, hg_lo)):
                            for h in range(2):
                                pool.dma_start(Mt[part * LH:(part + 1) * LH, b, h, :].bitcast(F32),
                                               rows[m][q * NB:(q + 1) * NB, :]).then_inc(hg_in[b], 16)
                for b in range(B):
                    pool.wait_ge(hg_in[b], 64 * (g + 1))
                    pool.sem_inc(hg_placed, 1)
            for k in range(3):
                pool.wait_ge(x_ready, NM * (k + 1))
                pool.wait_ge(brow_in, 16 * (2 if k < 2 else 3))
                if k == 2:
                    wait_drained(pool, ("Yr", 0, R - 1, NM - 1, 1))
                for m in range(NM):
                    ins = pool.tensor_tensor(xplus[k][m], xrows[:, m, :], brow[:, k % 2, :], ALU.add)
                    if m == NM - 1:
                        ins.then_inc(xplus_ready, 1)

        @block.tensor
        def _(pe):
            weight = [0]

            def next_weight(name):
                i = weight[0]
                assert WEIGHTS[i] == name, (WEIGHTS[i], name)
                pe.wait_ge(weight_in[weight_slot(i)], 16 * weight_uses(i))
                weight[0] += 1
                return wslot(i)

            def acquire(name):
                i = NUMBER[name]
                if i >= BANKS:
                    wait_drained(pe, TILES[i - BANKS][0])

            def rows_half(name, cols, w, m, h, extra=None):
                acquire(name)
                if extra is not None:
                    pe.matmul(psum(name, FH), extra[0], extra[1], start=True, stop=False)
                for c in range(FC):
                    mm = pe.matmul(psum(name, FH), cols(c, m), w[:, c, h * FH:(h + 1) * FH],
                                   start=(c == 0 and extra is None), stop=(c == FC - 1))
                mm.then_inc(tile_full, 1)
                return mm

            def cols_chunk(name, c, pairs):
                acquire(name)
                for k, (w, x) in enumerate(pairs):
                    mm = pe.matmul(psum(name, N), w[:, c * P:(c + 1) * P], x,
                                   start=(k == 0), stop=(k == len(pairs) - 1))
                mm.then_inc(tile_full, 1)

            def used():
                pe.drain().then_inc(weights_used, 1)

            def of(t):
                return lambda c, m: t[:, c, m * P:(m + 1) * P]

            def edge_chunk(c, u, first, last):
                pe.wait_ge(hot_ready, c + 1)
                for m in range(NM):
                    for h in range(2):
                        mm = pe.matmul(psum(("A", m, h), FH), hot[u][:, F + m * P:F + (m + 1) * P],
                                       hot[u][:, h * FH:(h + 1) * FH], start=first, stop=last,
                                       skip_group_check=True)
                mm.then_inc(hot_used, 1)
                return mm

            for u in range(HOT):
                edge_chunk(u, u, u == 0, False)
            with pe.Fori(1, EC // HOT - 1) as i:
                for u in range(HOT):
                    edge_chunk(i * HOT + u, u, False, False)
            for u in range(HOT):
                edge_chunk(EC - HOT + u, u, False, u == HOT - 1)
            pe.drain().then_inc(tile_full, 4)

            pe.wait_ge(q_in, 32)
            pe.wait_ge(const_made, 9)
            pe.wait_ge(small_in, 16 * 4)
            w = next_weight("WgT_q")
            for c4 in range(4):
                for h in range(2):
                    rows_half(("qg", c4, h), lambda c, m: qT[c // 3][:, c % 3, m * P:(m + 1) * P], w, c4, h,
                              (ones_row[:, :], bg_row[:, h * FH:(h + 1) * FH]))
            used()

            pe.wait_ge(graph_ready, 1)
            for s in range(NM):
                for r in range(R):
                    acquire(("AnT", s, r))
                    for m in range(NM):
                        mm = pe.transpose(psum(("AnT", s, r), N)[:, m * P:(m + 1) * P],
                                          AnS[:, m, r, s * P:(s + 1) * P], ident[:, :])
                    mm.then_inc(tile_full, 1)
            pe.wait_ge(graph_ready, 2)
            for s in range(NM):
                acquire(("AgT", s))
                for m in range(NM):
                    mm = pe.transpose(psum(("AgT", s), N)[:, m * P:(m + 1) * P],
                                      AgS[:, m, s * P:(s + 1) * P], ident[:, :])
                mm.then_inc(tile_full, 1)

            pe.wait_ge(x_in, 16)
            for g in range(2):
                x = (XT, HB)[g]
                if g == 1:
                    pe.wait_ge(h_out, FC)
                for r in range(R):
                    w = next_weight(f"Wrel{g + 1}_{r}")
                    for m in range(NM):
                        for h in range(2):
                            rows_half(("Y", g, r, m, h), of(x), w, m, h)
                    used()
                w = next_weight(f"Wroot{g + 1}")
                wait_drained(pe, ("Y", g, R - 1, NM - 1, 0), ("Y", g, R - 1, NM - 1, 1))
                if g == 0:
                    wait_drained(pe, ("AnT", 1, 0), ("AnT", 1, 1), ("AnT", 1, 2))
                for c in range(FC):
                    cols_chunk(("agg", g, c), c, [(w[:, k, :], x[:, k, :]) for k in range(FC)]
                               + [(Y[:, s, r, :], AnT[:, s, r, :]) for r in range(R) for s in range(NM)])
                used()
                w = next_weight("WgT_h")
                wait_drained(pe, ("agg", g, FC - 1), ("agg", g, FC - 2))
                for m in range(NM):
                    for h in range(2):
                        rows_half(("hg", g, m, h), of(HA), w, m, h)
                used()

                def gate_sum(b, j, t, k):
                    if j == 0:
                        pe.wait_ge(hg_placed, b + (B * g + 1))
                    pe.wait_ge(sig_ready, t - 1)
                    for n in range(3):
                        mm = pe.matmul(gsum[k % 2][:, n * 512:(n + 1) * 512], sel[:, j, :],
                                       Mt_graph[:, bass.ds(b, 1), n * 512:(n + 1) * 512], start=True, stop=True)
                    mm.then_inc(sum_ready, 1)

                def gate_reduce(b, u, j, t, k):
                    if j == 0:
                        pe.wait_ge(qi_copied, b + B * g)
                    pe.wait_ge(prod_ready, t + 1)
                    for c in range(FC):
                        for h in range(2):
                            mm = pe.matmul(gqi[u][:, c, j * NJ:(j + 1) * NJ],
                                           att[:, k % ATT, h, c * P:(c + 1) * P], ones4[:, :],
                                           start=(h == 0), stop=(h == 1))
                    mm.then_inc(prods_summed, 1)

                def gate_pair(i2, last):
                    for k in range(2 * JS):
                        if not (last and k == 2 * JS - 1):
                            k1 = k + 1
                            gate_sum(i2 * 2 + k1 // JS, k1 % JS, i2 * (2 * JS) + (STEPS * g + k1), k1)
                        gate_reduce(i2 * 2 + k // JS, k // JS, k % JS, i2 * (2 * JS) + (STEPS * g + k), k)

                wait_drained(pe, ("hg", g, NM - 1, 1))
                pe.wait_ge(sel_made, 4)
                if g == 0:
                    pe.wait_ge(qg_placed, 16 * 8)
                pe.wait_ge(hg_placed, B * g + 1)
                for n in range(3):
                    mm = pe.matmul(gsum[0][:, n * 512:(n + 1) * 512], sel[:, 0, :],
                                   Mt_graph[:, 0, n * 512:(n + 1) * 512], start=True, stop=True)
                mm.then_inc(sum_ready, 1)
                with pe.Fori(0, B // 2 - 1) as i2:
                    gate_pair(i2, False)
                gate_pair(B // 2 - 1, True)

                wh = next_weight("WqT_h")
                wq = next_weight("WqT_q")
                pe.wait_ge(qi_copied, B * (g + 1) + 1)
                for c in range(FC):
                    cols_chunk(("alpha", g, c), c, [(wh[:, k, :], HA[:, k, :]) for k in range(FC)]
                               + [(wq[:, k, :], qiT[:, k, :]) for k in range(FC)])
                used()
                used()

            pe.wait_ge(h_out, 2 * FC + 1)
            for m in range(NM):
                for h in range(2):
                    acquire(("back", m, h))
                    for c in range(3):
                        mm = pe.transpose(psum(("back", m, h), FH)[:, c * P:(c + 1) * P],
                                          HA[:, 3 * h + c, m * P:(m + 1) * P], ident[:, :])
                    mm.then_inc(tile_full, 1)

            def x_to_cols(k):
                pe.wait_ge(x_ready, NM * (k + 1))
                for c in range(FC):
                    acquire(("xT", k, c))
                    for m in range(NM):
                        mm = pe.transpose(psum(("xT", k, c), N)[:, m * P:(m + 1) * P],
                                          xrows[:, m, c * P:(c + 1) * P], ident[:, :])
                    mm.then_inc(tile_full, 1)
                wait_drained(pe, ("xT", k, FC - 1), ("xT", k, FC - 2))

            def gcn_product(k, name, x):
                w = next_weight(name)
                for m in range(NM):
                    for h in range(2):
                        rows_half(("Yg", k, m, h), of(x), w, m, h)
                used()
                wait_drained(pe, ("Yg", k, 1, 0), ("Yg", k, 1, 1))

            def gcn_rows(k, slot):
                for m in range(NM):
                    for h in range(2):
                        acquire(("out", k, m, h))
                        for s in range(NM):
                            mm = pe.matmul(psum(("out", k, m, h), FH), AgT[:, s, m * P:(m + 1) * P],
                                           Y[:, s, slot, h * FH:(h + 1) * FH], start=(s == 0), stop=(s == NM - 1))
                        mm.then_inc(tile_full, 1)

            def qk_weights(k):
                C = 2 * HEADS[k]
                acquire(("wqk", k))
                for r in range(R):
                    w = next_weight(f"W{k + 1}T_{r}")
                    for c in range(FC):
                        o = c * R * C + r * C
                        for f in range(FC):
                            mm = pe.matmul(psum(("wqk", k), 512)[:, o:o + C], w[:, f, c * P:(c + 1) * P],
                                           qk[k][:, f, :], start=(f == 0), stop=(f == FC - 1))
                    if r == R - 1:
                        mm.then_inc(tile_full, 1)
                    used()

            x_to_cols(0)
            gcn_product(0, "gcn1", HB)
            wait_drained(pe, ("AgT", 1))
            for c in range(FC):
                cols_chunk(("agg", 2, c), c, [(Y[:, s, 0, :], AgT[:, s, :]) for s in range(NM)])
            wait_drained(pe, ("agg", 2, FC - 1), ("agg", 2, FC - 2))
            gcn_product(1, "gcn2", HA)
            gcn_rows(0, 1)
            qk_weights(0)
            x_to_cols(1)
            gcn_product(2, "gcn3", HB)
            gcn_rows(1, 0)
            qk_weights(1)
            x_to_cols(2)

            for k in range(2):
                H, C = HEADS[k], 2 * HEADS[k]
                x = (HB, HA)[k]
                if k == 1:
                    pe.wait_ge(h_out, 2 * FC + 2)
                wait_drained(pe, ("wqk", k))
                acquire(("QN", k))
                for m in range(NM):
                    for c in range(FC):
                        mm = pe.matmul(psum(("QN", k), 512)[:, m * R * C:(m + 1) * R * C], x[:, c, m * P:(m + 1) * P],
                                       wqk[k][:, c, :], start=(c == 0), stop=(c == FC - 1))
                mm.then_inc(tile_full, 1)
                acquire(("KT", k))
                for c in range(FC):
                    mm = pe.matmul(psum(("KT", k), N, R * C), wqk[k][:, c, :], x[:, c, :],
                                   start=(c == 0), stop=(c == FC - 1))
                mm.then_inc(tile_full, 1)
                wait_drained(pe, ("KT", k))
                for i in range((H * R + 1) // 2):
                    acquire(("Kb", k, i))
                    for e in range(2 * i, min(2 * i + 2, H * R)):
                        col = (e % R) * C + H + e // R
                        mm = pe.matmul(psum(("Kb", k, i), 512)[:, (e % 2) * N:(e % 2 + 1) * N],
                                       ident[0:R * C, col:col + 1].broadcast_to([R * C, P]), KT[0:R * C, :],
                                       start=True, stop=True)
                    mm.then_inc(tile_full, 1)
                for r in range(R):
                    w = next_weight(f"W{k + 1}_{r}")
                    for m in range(NM):
                        for h in range(2):
                            rows_half(("Yr", k, r, m, h), of(x), w, m, h)
                    used()
                for m in range(NM):
                    for h in range(H):
                        pe.wait_ge(p_ready, k * NM * HEADS[0] + m * H + h + 1)
                        for s in range(NM):
                            name = ("PT", k, m, h, s)
                            acquire(name)
                            for r in range(R):
                                mm = pe.transpose(psum(name, FH)[:, r * P:(r + 1) * P],
                                                  U[:, m, h, r, s * P:(s + 1) * P], ident[:, :])
                            mm.then_inc(tile_full, 1)
                wait_drained(pe, ("PT", k, NM - 1, H - 1, 0), ("PT", k, NM - 1, H - 1, 1),
                             ("Yr", k, R - 1, NM - 1, 1))
                for m in range(NM):
                    for h in range(2):
                        name = ("att", m, h) if k == 0 else ("out", 2, m, h)
                        acquire(name)
                        D = F // H if k == 0 else FH
                        for e in range(FH // D):
                            head = (2 * h + e) if k == 0 else 0
                            f0 = h * FH + e * D
                            for n in range(R * NM):
                                mm = pe.matmul(psum(name, FH)[:, e * D:(e + 1) * D],
                                               PT[:, n % NM, head, n // NM, m * P:(m + 1) * P],
                                               Y[:, n % NM, n // NM, f0:f0 + D],
                                               start=(n == 0), stop=(n == R * NM - 1))
                        mm.then_inc(tile_full, 1)
                if k == 0:
                    wait_drained(pe, ("att", NM - 1, 1))
                    for c in range(FC):
                        acquire(("hT", c))
                        for m in range(NM):
                            mm = pe.transpose(psum(("hT", c), N)[:, m * P:(m + 1) * P],
                                              yrows[:, m, c * P:(c + 1) * P], ident[:, :])
                        mm.then_inc(tile_full, 1)

        @block.scalar
        def _(act):
            def drain_copy(name, dst, src):
                wait_full(act, name)
                act.activation(dst, src, ACT.Copy).then_inc(drained["A"], 1)

            for m in range(NM):
                drain_copy(("A", m, 0), Acnt[:, m, :, :].rearrange("p r n -> p (r n)")[:, 0:FH], psum(("A", m, 0), FH))
            act.wait_ge(deg_ready, 1)
            act.activation(cnt[:, :, 7], cnt[:, :, 3], ACT.Sqrt).then_inc(root_ready, 1)
            for c in range(4):
                for h in range(2):
                    wait_full(act, ("qg", c, h))
                    act.activation(qg_hi[:, c, h * FH:(h + 1) * FH].bitcast(F32R), psum(("qg", c, h), FH),
                                   ACT.Copy).then_inc(qg_hi_ready, 1)
            for g in range(2):
                if g == 0:
                    for s in range(NM):
                        for r in (0, 2):
                            drain_copy(("AnT", s, r), AnT[:, s, r, :], psum(("AnT", s, r), N))
                for r in range(R):
                    for m in range(NM):
                        drain_copy(("Y", g, r, m, 0), Y[:, m, r, 0:FH], psum(("Y", g, r, m, 0), FH))
                if g == 0:
                    act.wait_ge(small_in, 16 * 4)
                for c in range(0, FC, 2):
                    wait_full(act, ("agg", g, c))
                    act.activation(HA[:, c, :], psum(("agg", g, c), N), ACT.Relu,
                                   bias=bcol[:, g, c:c + 1]).then_inc(drained["A"], 1)
                for m in range(NM):
                    for h in range(2):
                        wait_full(act, ("hg", g, m, h))
                        act.activation(hg_hi[m][:, h * FH:(h + 1) * FH].bitcast(F32R), psum(("hg", g, m, h), FH),
                                       ACT.Copy).then_inc(hg_hi_ready, 1)
                with act.Fori(0, B // 2) as i2:
                    for k in range(2 * JS):
                        act.wait_ge(sum_ready, i2 * (2 * JS) + (STEPS * g + k + 1))
                        act.wait_ge(prods_summed, i2 * (2 * JS) + (STEPS * g + k + 1))
                        act.activation(att[:, k % ATT, :, :].rearrange("p h f -> p (h f)"), gsum[k % 2],
                                       ACT.Sigmoid).then_inc(sig_ready, 1)
                act.wait_ge(qi_copied, B * (g + 1) + 1)
                act.activation(TY[:, :], QX[:, :], ACT.Tanh).then_inc(tanh_ready, 1)
                for c in range(FC):
                    wait_full(act, ("alpha", g, c))
                    act.activation(alpha[:, c, :], psum(("alpha", g, c), N), ACT.Sigmoid,
                                   bias=bcol[:, 2, c:c + 1]).then_inc(drained["A"], 1)

            def layer_norm_std(k):
                for m in range(NM):
                    act.wait_ge(var_ready, NM * k + m + 1)
                    act.activation(mv[:, m, 2:3], mv[:, m, 1:2], ACT.Sqrt, bias=epsc[:, :]).then_inc(std_ready, 1)

            def drain_x(k):
                for c in range(0, FC, 2):
                    drain_copy(("xT", k, c), HB[:, c, :], psum(("xT", k, c), N))

            def drain_gcn(k, slot):
                for m in range(NM):
                    drain_copy(("Yg", k, m, 0), Y[:, m, slot, 0:FH], psum(("Yg", k, m, 0), FH))

            act.wait_ge(const_made, 9)
            layer_norm_std(0)
            drain_x(0)
            drain_gcn(0, 0)
            for c in range(0, FC, 2):
                wait_full(act, ("agg", 2, c))
                act.activation(HA[:, c, :], psum(("agg", 2, c), N), ACT.Relu,
                               bias=bcol[:, 3, c:c + 1]).then_inc(drained["A"], 1)
            drain_gcn(1, 1)
            layer_norm_std(1)
            drain_copy(("wqk", 0), wqk[0][:, :, :].rearrange("p c n -> p (c n)"), psum(("wqk", 0), FC * R * 2 * HEADS[0]))
            drain_x(1)
            drain_gcn(2, 0)
            layer_norm_std(2)
            drain_copy(("wqk", 1), wqk[1][:, :, :].rearrange("p c n -> p (c n)"), psum(("wqk", 1), FC * R * 2 * HEADS[1]))
            drain_x(2)
            for k in range(2):
                H, C = HEADS[k], 2 * HEADS[k]
                drain_copy(("QN", k), QN[:, :, 0:R * C], psum(("QN", k), NM * R * C).rearrange("p (m c) -> p m c", m=NM))
                drain_copy(("KT", k), KT[0:R * C, :], psum(("KT", k), N, R * C))
                wait_drained(act, ("KT", k))
                for i in range((H * R + 1) // 2):
                    wait_full(act, ("Kb", k, i))
                    for e in range(2 * i, min(2 * i + 2, H * R)):
                        h, r = e // R, e % R
                        for m in range(NM):
                            ins = act.activation(U[:, m, h, r, :], psum(("Kb", k, i), 512)[:, (e % 2) * N:(e % 2 + 1) * N],
                                                 ACT.Identity, bias=QN[:, m, r * C + h:r * C + h + 1])
                    ins.then_inc(drained["A"], 1)

                def exps(m):
                    act.wait_ge(nmax_ready, NM * k + m + 1)
                    for h in range(H):
                        v = U[:, m, h, :, :].rearrange("p r n -> p (r n)")
                        act.activation(v, v, ACT.Exp, bias=smx[:, m, 1, h:h + 1]).then_inc(e_ready, 1)

                for r in range(R):
                    for m in range(NM):
                        for h in range(2):
                            drain_copy(("Yr", k, r, m, h), Y[:, m, r, h * FH:(h + 1) * FH], psum(("Yr", k, r, m, h), FH))
                    if r < NM:
                        exps(r)
                for m in range(NM):
                    for h in range(H):
                        drain_copy(("PT", k, m, h, 0), PT[:, 0, h, :, m * P:(m + 1) * P],
                                   psum(("PT", k, m, h, 0), FH).rearrange("p (r n) -> p r n", r=R))
                if k == 0:
                    for c in range(FC):
                        wait_full(act, ("hT", c))
                        act.activation(HA[:, c, :], psum(("hT", c), N), ACT.Identity,
                                       bias=bcol[:, 4, c:c + 1]).then_inc(drained["A"], 1)
                    act.wait_ge(elu_min, 1)
                    act.activation(elu_m, elu_m, ACT.Exp).then_inc(elu_exp, 1)
            layer_norm_std(3)

        @block.vector
        def _(dve):
            links = [0]

            def link(ins):
                links[0] += 1
                ins.then_inc(dve_chain, 1)
                dve.wait_ge(dve_chain, links[0])

            def drain_copy(name, dst, src):
                wait_full(dve, name)
                dve.tensor_copy(dst, src).then_inc(drained["V"], 1)

            dve.sem_inc(qi_copied, 1)
            dve.wait_ge(ints_in, 48)
            dve.wait_ge(iota_made, 1)
            dve.tensor_copy(iota_h, iota_i)
            link(dve.tensor_copy(idxf[:, :, :], idx[:, :, :]))
            link(dve.scalar_tensor_tensor(out=comb[:, :], in0=idxf[:, 2, :], scalar=float(N), in1=idxf[:, 1, :],
                                          op0=ALU.mult, op1=ALU.add))

            def one_hots(c, u, wait):
                if wait:
                    dve.wait_ge(hot_used, c - (HOT - 1))
                dve.tensor_scalar(hot[u][:, 0:F], iota_h, comb[:, bass.ds(c, 1)], None, ALU.is_equal)
                dve.tensor_scalar(hot[u][:, F:F + N], iota_h[:, 0:N], idxf[:, 0, bass.ds(c, 1)], None,
                                  ALU.is_equal).then_inc(hot_ready, 1)

            for u in range(HOT):
                one_hots(u, u, False)
            with dve.Fori(1, EC // HOT) as i:
                for u in range(HOT):
                    one_hots(i * HOT + u, u, True)

            dve.wait_ge(const_made, 9)
            v = sel[:, :, :].rearrange("p j (n l) -> p j n l", n=NJ)
            for part in range(2):
                p0 = part * LH
                dve.tensor_copy(v[p0:p0 + LH], ident[p0:p0 + LH, p0:p0 + LH].unsqueeze(1).unsqueeze(1).broadcast_to(
                    [LH, JS, NJ, LH])).then_inc(sel_made, 1)
                p0 = (2 + part) * LH
                dve.tensor_copy(sel[p0:p0 + LH, :, :].rearrange("p j (n l) -> p (j n) l", n=NJ),
                                ident[p0:p0 + LH, p0:p0 + LH].unsqueeze(2).broadcast_to([LH, NB, LH])).then_inc(
                    sel_made, 1)

            for m in range(NM):
                drain_copy(("A", m, 1), Acnt[:, m, :, :].rearrange("p r n -> p (r n)")[:, FH:F], psum(("A", m, 1), FH))
            wait_drained(dve, ("A", 1, 0), ("A", 1, 1))
            link(dve.tensor_reduce(cnt[:, :, 0:R], Acnt[:, :, :, :], AX.X, ALU.add))
            link(dve.tensor_reduce(cnt[:, :, 3:4], cnt[:, :, 0:R], AX.X, ALU.add))
            dve.tensor_scalar(cnt[:, :, 3:4], cnt[:, :, 3:4], 1.0, None, ALU.add).then_inc(deg_ready, 1)
            link(dve.tensor_scalar(cnt[:, :, 4:7], cnt[:, :, 0:R], 1.0, None, ALU.max))
            link(dve.reciprocal(cnt[:, :, 4:7], cnt[:, :, 4:7]))
            for m in range(NM):
                for r in range(R):
                    ins = dve.tensor_scalar(AnS[:, m, r, :], Acnt[:, m, r, :], cnt[:, m, 4 + r:5 + r], None, ALU.mult)
            ins.then_inc(graph_ready, 1)
            link(dve.tensor_tensor(AgS, Acnt[:, :, 0, :], Acnt[:, :, 1, :], ALU.add))
            link(dve.tensor_tensor(AgS, AgS, Acnt[:, :, 2, :], ALU.add))
            for m in range(NM):
                d = AgS[:, m, m * P:(m + 1) * P]
                link(dve.tensor_tensor(d, d, ident[:, :], ALU.add))
            dve.wait_ge(root_ready, 1)
            link(dve.reciprocal(cnt[:, :, 7], cnt[:, :, 7]))
            for m in range(NM):
                ins = dve.tensor_scalar(AgS[:, m, :], AgS[:, m, :], cnt[:, m, 7:8], None, ALU.mult)
            ins.then_inc(graph_ready, 1)

            for c in range(4):
                for h in range(2):
                    dve.wait_ge(qg_hi_ready, 2 * c + h + 1)
                    f = slice(h * FH, (h + 1) * FH)
                    dve.tensor_tensor(qg_lo[:, c, f].bitcast(F32R), psum(("qg", c, h), FH), qg_hi[:, c, f],
                                      ALU.subtract).then_inc(drained["V"], 1)
            for g in range(2):
                if g == 0:
                    for s in range(NM):
                        drain_copy(("AnT", s, 1), AnT[:, s, 1, :], psum(("AnT", s, 1), N))
                    for s in range(NM):
                        wait_full(dve, ("AgT", s))
                        dve.tensor_scalar(AgT[:, s, :], psum(("AgT", s), N), cnt[:, s, 7:8], None, ALU.mult).then_inc(
                            drained["V"], 1)
                for r in range(R):
                    for m in range(NM):
                        drain_copy(("Y", g, r, m, 1), Y[:, m, r, FH:F], psum(("Y", g, r, m, 1), FH))
                if g == 0:
                    dve.wait_ge(small_in, 16 * 4)
                for c in range(1, FC, 2):
                    wait_full(dve, ("agg", g, c))
                    dve.tensor_scalar(HA[:, c, :], psum(("agg", g, c), N), bcol[:, g, c:c + 1], 0.0, ALU.add,
                                      ALU.max).then_inc(drained["V"], 1)
                for m in range(NM):
                    for h in range(2):
                        dve.wait_ge(hg_hi_ready, 4 * g + 2 * m + h + 1)
                        f = slice(h * FH, (h + 1) * FH)
                        dve.tensor_tensor(hg_lo[m][:, f].bitcast(F32R), psum(("hg", g, m, h), FH), hg_hi[m][:, f],
                                          ALU.subtract).then_inc(drained["V"], 1)

                def copy_qi(b, u, t):
                    dve.wait_ge(prods_summed, t + (ATT + 1))
                    dve.tensor_copy(qiT[:, :, bass.ds(b * NB, NB)], gqi[u]).then_inc(qi_copied, 1)

                def products(i2, first):
                    for k in range(2 * JS):
                        u = k // JS
                        if k % JS == 0:
                            dve.wait_ge(qrep_in[u], i2 * (16 * NJ) + 16 * NJ * (B // 2 * g + 1))
                        dve.wait_ge(sig_ready, i2 * (2 * JS) + (STEPS * g + k + 1))
                        v = att[:, k % ATT, :, :]
                        dve.tensor_tensor(v, v, qrep[:, u, :, :], ALU.mult).then_inc(prod_ready, 1)
                        if k % JS == 1 and not (first and u == 0):
                            copy_qi(i2 * 2 + (u - 1), 1 - u, i2 * (2 * JS) + (STEPS * g + JS * u - 1))

                products(0, True)
                with dve.Fori(1, B // 2) as i2:
                    products(i2, False)
                copy_qi(B - 1, 1, STEPS * (g + 1) - 1)
                dve.wait_ge(tanh_ready, g + 1)
                link(dve.tensor_tensor(thT, thT, HA[:, :, :], ALU.subtract))
                for c in range(FC):
                    wait_drained(dve, ("alpha", g, c))
                    link(dve.tensor_tensor(alpha[:, c, :], alpha[:, c, :], thT[:, c, :], ALU.mult))
                    dve.tensor_tensor(HB[:, c, :], alpha[:, c, :], HA[:, c, :], ALU.add).then_inc(h_out, 1)
            dve.wait_ge(h_out, 2 * FC)
            dve.tensor_tensor(HA[:, :, :], HB[:, :, :], XT[:, :, :], ALU.add).then_inc(h_out, 1)

            def layer_norm(k, source, drains):
                for m in range(NM):
                    for h in range(2):
                        if drains:
                            wait_full(dve, ("back", m, h))
                        link(dve.bn_stats(stat[:, m, h, :], source(m, h)))
                    dve.bn_aggr(mv[:, m, 0:2], stat[:, m, :, :]).then_inc(var_ready, 1)
                for m in range(NM):
                    dve.wait_ge(std_ready, NM * k + m + 1)
                    link(dve.reciprocal(mv[:, m, 3:4], mv[:, m, 2:3]))
                    for h in range(2):
                        ins = dve.tensor_scalar(xrows[:, m, h * FH:(h + 1) * FH], source(m, h), mv[:, m, 0:1],
                                                mv[:, m, 3:4], ALU.subtract, ALU.mult)
                        if drains:
                            ins.then_inc(drained["V"], 1)
                    if drains:
                        dve.wait_ge(drained["V"], DRAINS[("back", m, 1)])
                        dve.drain().then_inc(x_ready, 1)
                    else:
                        ins.then_inc(x_ready, 1)

            def y_half(m, h):
                return yrows[:, m, h * FH:(h + 1) * FH]

            def drain_x(k):
                for c in range(1, FC, 2):
                    drain_copy(("xT", k, c), HB[:, c, :], psum(("xT", k, c), N))

            def drain_gcn(k, slot):
                for m in range(NM):
                    drain_copy(("Yg", k, m, 1), Y[:, m, slot, FH:F], psum(("Yg", k, m, 1), FH))

            def residual(k):
                dve.wait_ge(xplus_ready, k + 1)
                for m in range(NM):
                    for h in range(2):
                        wait_full(dve, ("out", k, m, h))
                        dve.tensor_tensor(y_half(m, h), psum(("out", k, m, h), FH), xplus[k][m][:, h * FH:(h + 1) * FH],
                                          ALU.add).then_inc(drained["V"], 1)
                wait_drained(dve, ("out", k, 1, 1))

            layer_norm(0, lambda m, h: psum(("back", m, h), FH), True)
            drain_x(0)
            dve.tensor_scalar(hide[:, :, :, :], Acnt[:, :, :, :], 0.0, -BIG, ALU.is_equal, ALU.mult)
            drain_gcn(0, 0)
            for c in range(1, FC, 2):
                wait_full(dve, ("agg", 2, c))
                dve.tensor_scalar(HA[:, c, :], psum(("agg", 2, c), N), bcol[:, 3, c:c + 1], 0.0, ALU.add,
                                  ALU.max).then_inc(drained["V"], 1)
            drain_gcn(1, 1)
            residual(0)
            layer_norm(1, y_half, False)
            drain_x(1)
            drain_gcn(2, 0)
            residual(1)
            layer_norm(2, y_half, False)
            drain_x(2)
            for k in range(2):
                H, C = HEADS[k], 2 * HEADS[k]
                wait_drained(dve, ("Kb", k, (H * R + 1) // 2 - 1))
                for m in range(NM):
                    v = U[:, m, 0:H, :, :].rearrange("p h r n -> p (h r n)")
                    link(dve.scalar_tensor_tensor(out=v, in0=v, scalar=SLOPE, in1=v, op0=ALU.mult, op1=ALU.max))
                    for h in range(H):
                        v = U[:, m, h, :, :].rearrange("p r n -> p (r n)")
                        ins = dve.tensor_tensor_reduce(v, v, hide[:, m, :, :].rearrange("p r n -> p (r n)"), 1.0,
                                                       -3e38, ALU.add, ALU.max, smx[:, m, 0, h:h + 1])
                    link(ins)
                    dve.tensor_scalar(smx[:, m, 1, 0:H], smx[:, m, 0, 0:H], -1.0, None, ALU.mult).then_inc(nmax_ready, 1)
                for m in range(NM):
                    for h in range(H):
                        dve.wait_ge(e_ready, k * NM * HEADS[0] + m * H + h + 1)
                        v = U[:, m, h, :, :].rearrange("p r n -> p (r n)")
                        ins = dve.tensor_tensor_reduce(v, v, Acnt[:, m, :, :].rearrange("p r n -> p (r n)"), 1.0,
                                                       0.0, ALU.mult, ALU.add, smx[:, m, 2, h:h + 1])
                        ins.then_inc(p_ready, 1)
                    dve.wait_ge(p_ready, k * NM * HEADS[0] + (m + 1) * H)
                    link(dve.tensor_scalar(smx[:, m, 3, 0:H], smx[:, m, 2, 0:H], EPS_Z, None, ALU.add))
                    link(dve.reciprocal(smx[:, m, 3, 0:H], smx[:, m, 3, 0:H]))
                for m in range(NM):
                    for h in range(H):
                        drain_copy(("PT", k, m, h, 1), PT[:, 1, h, :, m * P:(m + 1) * P],
                                   psum(("PT", k, m, h, 1), FH).rearrange("p (r n) -> p r n", r=R))
                if k == 0:
                    D = F // H
                    for m in range(NM):
                        for h in range(2):
                            wait_full(dve, ("att", m, h))
                            for e in range(2):
                                head = 2 * h + e
                                ins = dve.tensor_scalar(yrows[:, m, head * D:(head + 1) * D],
                                                        psum(("att", m, h), FH)[:, e * D:(e + 1) * D],
                                                        smx[:, m, 3, head:head + 1], None, ALU.mult)
                            ins.then_inc(drained["V"], 1)
                    wait_drained(dve, ("hT", FC - 1))
                    t = flat(HA)
                    dve.tensor_scalar(elu_m, t, 0.0, None, ALU.min).then_inc(elu_min, 1)
                    dve.wait_ge(elu_min, 1)
                    link(dve.tensor_scalar(t, t, 0.0, -1.0, ALU.max, ALU.add))
                    dve.wait_ge(elu_exp, 1)
                    dve.tensor_tensor(t, t, elu_m, ALU.add).then_inc(h_out, 1)
                else:
                    dve.wait_ge(xplus_ready, 3)
                    for m in range(NM):
                        for h in range(2):
                            wait_full(dve, ("out", 2, m, h))
                            dve.scalar_tensor_tensor(out=y_half(m, h), in0=psum(("out", 2, m, h), FH),
                                                     scalar=smx[:, m, 3, 0:1],
                                                     in1=xplus[2][m][:, h * FH:(h + 1) * FH],
                                                     op0=ALU.mult, op1=ALU.add).then_inc(drained["V"], 1)
                    wait_drained(dve, ("out", 2, 1, 1))
            layer_norm(3, y_half, False)


def kernel(**inputs):
    import numpy as np
    import concourse.bacc as bacc
    from concourse import mybir as mb
    from concourse.bass_utils import run_bass_kernel_spmd as run

    def cols(w):
        return np.ascontiguousarray(np.transpose(w))

    def chunks(v):
        return np.ascontiguousarray(np.swapaxes(v.reshape(FC, P, -1), 0, 1))

    v = {k: np.asarray(x) for k, x in inputs.items()}
    q = v["L0_gnn_query_embs"].reshape(B * L, F)
    arrays = {
        "dst": v["dst"], "src": v["src"], "etype": v["edge_type_3"],
        "xT": cols(v["x"]), "q": q, "qT": cols(q), "bg": v["L0_gnn_bg"].reshape(1, F),
        "bias_cols": np.ascontiguousarray(np.stack([v[n].reshape(FC, P).T for n in (
            "L0_gnn_b1", "L0_gnn_b2", "L0_gnn_bq", "L1_gnn_b1", "L3_gnn_b1")], axis=1)),
        "brow0": v["L1_gnn_b2"], "brow1": v["L2_gnn_b"], "brow2": v["L3_gnn_b2"],
        "qk0": chunks(np.concatenate([v["L3_gnn_q1"], v["L3_gnn_k1"]], axis=1)),
        "qk1": chunks(np.concatenate([v["L3_gnn_q2"], v["L3_gnn_k2"]], axis=1)),
        "WgT_h": cols(v["L0_gnn_Wg"][:, :F]), "WgT_q": cols(v["L0_gnn_Wg"][:, F:]),
        "WqT_h": cols(v["L0_gnn_Wq"][:, :F]), "WqT_q": cols(v["L0_gnn_Wq"][:, F:]),
        "Wroot1": v["L0_gnn_W_root1"], "Wroot2": v["L0_gnn_W_root2"],
        "gcn1": v["L1_gnn_W1"], "gcn2": v["L1_gnn_W2"], "gcn3": v["L2_gnn_W"],
    }
    for r in range(R):
        arrays[f"Wrel1_{r}"] = v["L0_gnn_W_rel1"][r]
        arrays[f"Wrel2_{r}"] = v["L0_gnn_W_rel2"][r]
        arrays[f"W1_{r}"], arrays[f"W1T_{r}"] = v["L3_gnn_W1"][r], cols(v["L3_gnn_W1"][r])
        arrays[f"W2_{r}"], arrays[f"W2T_{r}"] = v["L3_gnn_W2"][r], cols(v["L3_gnn_W2"][r])
    arrays = {k: np.ascontiguousarray(x) for k, x in arrays.items()}
    nc = bacc.Bacc("TRN2", target_bir_lowering=False, num_devices=1)
    a = {k: nc.dram_tensor(f"in_{k}", x.shape, mb.dt.from_np(x.dtype), kind="ExternalInput").ap()
         for k, x in arrays.items()}
    out = nc.dram_tensor("out_x", (N, F), mb.dt.float32, kind="ExternalOutput").ap()
    build(nc, a, out)
    r = run(nc, [{f"in_{k}": x for k, x in arrays.items()}], core_ids=[0])
    return r.results[0]["out_x"]
```

```python
from contextlib import ExitStack

import concourse.bass as bass
from concourse import mybir

P = 128
N = 256
NM = N // P
F = 768
FC = F // P
FH = F // 2
E = 4096
EC = E // P
R = 3
B = 8
NB = N // B
L = 64
LH = 32
NJ = 4
JS = NB // NJ
STEPS = B * JS
HEADS = (4, 1)
BANKS = 8
RING_PRE = 3
RING_POST = 5
HOT = 4
ATT = 4
LAG = 3
CHUNKS = (slice(0, 512), slice(512, 2 * F))
REDS = STEPS + LAG
BIG = 1e30
EPS = 1e-5
EPS_Z = 1e-16
SLOPE = 0.2

ALU = mybir.AluOpType
ACT = mybir.ActivationFunctionType
AX = mybir.AxisListType
F32 = mybir.dt.float32
F32R = mybir.dt.float32r
F16 = mybir.dt.float16
BF16 = mybir.dt.bfloat16
I32 = mybir.dt.int32

WEIGHTS = ["WgT_q"]
GATE_AT = []
for _g in range(2):
    WEIGHTS += [f"Wrel{_g + 1}_{_r}" for _r in range(R)] + [f"Wroot{_g + 1}", "WgT_h"]
    WEIGHTS += [f"W{_g + 1}T_{_r}" for _r in range(R)]
    GATE_AT.append(len(WEIGHTS))
    WEIGHTS += ["WqT_h", "WqT_q"]
PRE = len(WEIGHTS)
WEIGHTS += ["gcn1", "gcn2", "gcn3"] + [f"W1_{_r}" for _r in range(R)] + [f"W2_{_r}" for _r in range(R)]


def weight_slot(i):
    return i % RING_PRE if i < PRE else (i - PRE) % RING_POST


def weight_before(i):
    for k in range(i - 1, -1, -1):
        if weight_slot(k) == weight_slot(i):
            return k
    return None


def weight_uses(i):
    return sum(weight_slot(k) == weight_slot(i) for k in range(i + 1))


def plan_tiles():
    t = [(("A", m, h), "AV"[h]) for m in range(NM) for h in range(2)]
    t += [(("qg", c, h), "V") for c in range(4) for h in range(2)]
    for g in range(2):
        if g == 0:
            t += [(("AnT", s, r), "AV"[r % 2]) for s in range(NM) for r in range(R)]
            t += [(("AgT", s), "V") for s in range(NM)]
        t += [(("Y", g, r, m, h), "AV"[h]) for r in range(R) for m in range(NM) for h in range(2)]
        t += [(("agg", g, c), "AV"[c % 2]) for c in range(FC)]
        t += [(("hg", g, m, h), "V") for m in range(NM) for h in range(2)]
        t += [(("wqk", g), "A")]
        t += [(("qiT", g, c), "AV"[c % 2]) for c in range(FC)]
        t += [(("alpha", g, c), "A") for c in range(FC)]
    t += [(("back", m, h), "V") for m in range(NM) for h in range(2)]
    t += [(("xT", 0, c), "AV"[c % 2]) for c in range(FC)]
    t += [(("Yg", 0, m, h), "AV"[h]) for m in range(NM) for h in range(2)]
    t += [(("agg", 2, c), "AV"[c % 2]) for c in range(FC)]
    t += [(("Yg", 1, m, h), "AV"[h]) for m in range(NM) for h in range(2)]
    t += [(("out", 0, m, h), "V") for m in range(NM) for h in range(2)]
    t += [(("xT", 1, c), "AV"[c % 2]) for c in range(FC)]
    t += [(("Yg", 2, m, h), "AV"[h]) for m in range(NM) for h in range(2)]
    t += [(("out", 1, m, h), "V") for m in range(NM) for h in range(2)]
    t += [(("xT", 2, c), "AV"[c % 2]) for c in range(FC)]
    for k in range(2):
        t += [(("QN", k), "A"), (("KT", k), "A")]
        t += [(("Kb", k, i), "A") for i in range((HEADS[k] * R + 1) // 2)]
        t += [(("Yr", k, r, m, h), "A") for r in range(R) for m in range(NM) for h in range(2)]
        t += [(("PT", k, m, h, s), "AV"[s]) for m in range(NM) for h in range(HEADS[k]) for s in range(NM)]
        if k == 0:
            t += [(("att", m, h), "V") for m in range(NM) for h in range(2)]
            t += [(("hT", c), "A") for c in range(FC)]
        else:
            t += [(("out", 2, m, h), "V") for m in range(NM) for h in range(2)]
    return t


TILES = plan_tiles()
NUMBER = {name: i for i, (name, _) in enumerate(TILES)}
DRAINS = {name: sum(e == TILES[i][1] for _, e in TILES[:i + 1]) for name, i in NUMBER.items()}


def build(nc, a, out):
    ctx = ExitStack()
    with ctx:
        def sem(name):
            return ctx.enter_context(nc.semaphore(name))

        def sb(name, shape, dt=F32, stack=ctx):
            return stack.enter_context(nc.sbuf_tensor(name, shape, dt))

        W = sb("weight_slots", [P, RING_PRE, FC, F])
        HA = sb("colsA", [P, FC, N])
        HB = sb("colsB", [P, FC, N])
        XT = sb("x_cols", [P, FC, N])
        QX = sb("qi_cols_or_x_rows", [P, NM * F])
        TY = sb("tanh_cols_or_y_rows", [P, NM * F])
        Y = sb("products", [P, NM, R, F])
        Acnt = sb("edge_counts", [P, NM, R, N])
        AnT = sb("mean_weights_T", [P, NM, R, N])
        AgT = sb("gcn_weights_T", [P, NM, N])
        ident = sb("ident", [P, P])
        sel = sb("gate_select", [P, JS, P], F32R)
        window = sb("ones_window", [P, 2 * P])
        bcol = sb("bias_cols", [P, 5, FC])
        qk = [sb(f"qk{k}", [P, FC, 2 * HEADS[k]]) for k in range(2)]
        wqk = [sb(f"wqk{k}", [P, FC, R * 2 * HEADS[k]]) for k in range(2)]
        QN = sb("q_of_node", [P, NM, R * 2 * HEADS[0]])
        KT = window[0:R * 2 * HEADS[0], :]
        idxf = sb("edge_floats", [P, 3, EC])
        comb = sb("edge_rel_src", [P, EC])
        cnt = sb("counts", [P, NM, 8])
        stat = sb("bn_stats", [P, NM, 2, 6])
        mv = sb("mean_var", [P, NM, 4])
        smx = sb("softmax_small", [P, NM, 4, HEADS[0]])
        epsc = sb("eps", [P, 1])

        early, late = ExitStack(), ExitStack()
        Mt = sb("gate_moving", [P, B, 2, F], F32R, early)
        qrep = sb("q_replicated", [P, 2, 2, F], F32, early)
        att = sb("gate_products", [P, ATT, 2, F], F32, early)
        early.close()
        Wx = sb("weight_slots_late", [P, RING_POST - RING_PRE, FC, F], F32, late)
        U = sb("edge_scores", [P, NM, HEADS[0], R, N], F32, late)
        PT = sb("edge_weights_T", [P, NM, HEADS[0], R, N], F32, late)
        late.close()

        def flat(t):
            return t[:, :, :].rearrange("p c n -> p (c n)")

        hot = [Y[:, 0, :, :].rearrange("p r f -> p (r f)").bitcast(BF16)[:, 1024 * i:1024 * (i + 1)]
               for i in range(HOT)]
        iota_i = flat(HA)[:, 0:F].bitcast(I32)
        iota_h = flat(HB)[:, 0:F // 2].bitcast(F16)
        spare = AnT[:, :, :, :].rearrange("p m r n -> p (m r n)")
        bg_row, ones_row = spare[0:1, 0:F], spare[0:1, F:F + P]
        idx = spare[:, F + P:F + P + 3 * EC].bitcast(I32).rearrange("p (k c) -> p k c", k=3)
        qT = [t[:, :].rearrange("p (c l) -> p c l", c=FC // 2) for t in (QX, TY)]
        qg_hi = att[:, 0:2, :, :].rearrange("p a h f -> p (a h) f")
        qg_lo = att[:, 2:4, :, :].rearrange("p a h f -> p (a h) f")
        AnS = flat(HA).rearrange("p (m r n) -> p m r n", m=NM, r=R)
        AgS = flat(HB)[:, F:F + NM * N].rearrange("p (m n) -> p m n", m=NM)
        hg_hi = [Y[:, 0, m, :] for m in range(NM)]
        hg_lo = [Y[:, 1, m, :] for m in range(NM)]
        qiT = QX[:, :].rearrange("p (c n) -> p c n", c=FC)
        thT = TY[:, :].rearrange("p (c n) -> p c n", c=FC)
        alpha = att[:, 0, :, :].rearrange("p h f -> p (h f)").rearrange("p (c n) -> p c n", c=FC)
        xrows = QX[:, :].rearrange("p (m f) -> p m f", m=NM)
        yrows = TY[:, :].rearrange("p (m f) -> p m f", m=NM)
        brow = flat(XT).rearrange("p (m f) -> p m f", m=NM)
        xplus = [[Y[:, m, 2, :] for m in range(NM)]] * 2 + [
            [flat(HB)[:, m * F:(m + 1) * F] for m in range(NM)]]
        hide = AnT
        elu_m = U[:, 0, 0:2, :, :].rearrange("p h r n -> p (h r n)")
        att_flat = [att[:, i, :, :].rearrange("p h f -> p (h f)") for i in range(ATT)]
        qrep_flat = [qrep[:, u, :, :].rearrange("p h f -> p (h f)") for u in range(2)]
        Mt_graph = Mt[:, :, :, :].rearrange("p b h f -> p b (h f)")

        ps = ctx.enter_context(nc.psum_tensor("ps", [P, BANKS, 512], F32))
        gsum = [ps[:, 3 * i:3 * i + 3, :].rearrange("p b n -> p (b n)") for i in range(2)]
        gqi = [ps[:, 6 + h, 0:FH] for h in range(2)]

        def wslot(i):
            s = weight_slot(i)
            return W[:, s, :, :] if s < RING_PRE else Wx[:, s - RING_PRE, :, :]

        def psum(name, width, parts=P):
            return ps[0:parts, NUMBER[name] % BANKS, 0:width]

        tile_full = sem("tile_full")
        drained = {"A": sem("drained_by_act"), "V": sem("drained_by_dve")}
        weight_in = [sem(f"weight_in{s}") for s in range(RING_POST)]
        weights_used = sem("weights_used")
        ints_in = sem("ints_in")
        x_in = sem("x_in")
        q_in = sem("q_in")
        small_in = sem("small_in")
        const_made = sem("const_made")
        iota_made = sem("iota_made")
        sel_made = sem("sel_made")
        hot_ready = sem("hot_ready")
        hot_used = sem("hot_used")
        deg_ready = sem("deg_ready")
        root_ready = sem("root_ready")
        graph_ready = sem("graph_ready")
        qg_hi_ready = sem("qg_hi_ready")
        qg_placed = sem("qg_placed")
        hg_hi_ready = sem("hg_hi_ready")
        hg_in = [[sem(f"hg_{part}_in{b}") for b in range(B)] for part in ("hi", "lo")]
        hg_placed = sem("hg_placed")
        qrep_in = [sem(f"qrep_in{u}") for u in range(2)]
        sum_ready = sem("sum_ready")
        sig_ready = sem("sig_ready")
        prod_ready = sem("prod_ready")
        halves_added = sem("halves_added")
        prods_summed = sem("prods_summed")
        qi_rows = sem("qi_rows")
        tanh_ready = sem("tanh_ready")
        h_out = sem("h_out")
        dve_chain = sem("dve_chain")
        var_ready = sem("var_ready")
        std_ready = sem("std_ready")
        x_ready = sem("x_ready")
        brow_in = sem("brow_in")
        xplus_ready = sem("xplus_ready")
        u_ready = sem("u_ready")
        nmax_ready = sem("nmax_ready")
        e_ready = sem("e_ready")
        p_ready = sem("p_ready")
        elu_min = sem("elu_min")
        elu_exp = sem("elu_exp")
        out_done = sem("out_done")

        block = ctx.enter_context(nc.Block())

        def wait_drained(eng, *names):
            most = {}
            for name in names:
                e = TILES[NUMBER[name]][1]
                most[e] = max(most.get(e, 0), DRAINS[name])
            for e, n in most.items():
                eng.wait_ge(drained[e], n)

        def wait_full(eng, name):
            eng.wait_ge(tile_full, NUMBER[name] + 1)

        def place_hg(queue, m, part):
            rows = (hg_hi, hg_lo)[part][m]
            for q in range(B // NM):
                b = m * (B // NM) + q
                queue.dma_start(Mt[(2 + part) * LH:(3 + part) * LH, b, :, :].bitcast(F32),
                                rows[q * NB:(q + 1) * NB, :].unsqueeze(1).broadcast_to([NB, 2, F])).then_inc(hg_in[part][b], 16)

        @block.sync
        def _(sp):
            for k, name in enumerate(("dst", "src", "etype")):
                sp.dma_start(idx[:, k, :], a[name].rearrange("(p c) -> p c", p=P)).then_inc(ints_in, 16)

            def load(i):
                before = weight_before(i)
                if before is not None:
                    sp.wait_ge(weights_used, before + 1)
                sp.dma_start(wslot(i), a[WEIGHTS[i]].rearrange("(c p) n -> p c n", p=P)).then_inc(
                    weight_in[weight_slot(i)], 16)

            qT_rows = a["qT"].rearrange("(c p) n -> p c n", p=P)
            for k in range(2):
                sp.dma_start(qT[k], qT_rows[:, 3 * k:3 * k + 3, :]).then_inc(q_in, 16)
            sp.dma_start(bg_row[:, :], a["bg"]).then_inc(small_in, 16)
            load(0)
            sp.dma_start(XT[:, :, :], a["xT"].rearrange("(c p) n -> p c n", p=P)).then_inc(x_in, 16)
            load(1)
            sp.dma_start(bcol[:, :, :], a["bias_cols"]).then_inc(small_in, 16)
            for k in range(2):
                sp.dma_start(qk[k][:, :, :], a[f"qk{k}"]).then_inc(small_in, 16)

            q_rows = a["q"].rearrange("(b h l) f -> b l h f", h=2, l=LH)

            def place_q(g, b, u):
                for n in range(NJ):
                    sp.dma_start(qrep[n * LH:(n + 1) * LH, u, :, :],
                                 q_rows[bass.ds(b, 1), :, :, :].rearrange("o l h f -> (o l) h f")).then_inc(
                        qrep_in[u], 16)

            at = 2
            for g in range(2):
                for u in range(2):
                    if g == 1:
                        sp.wait_ge(prod_ready, 4 + 2 * (STEPS + JS * (u - 1)))
                    place_q(g, u, u)
                while at < GATE_AT[g]:
                    load(at)
                    at += 1
                for m in range(NM):
                    wait_drained(sp, ("hg", g, m, 1))
                    place_hg(sp, m, 0)
                while weight_before(at) < GATE_AT[g]:
                    load(at)
                    at += 1
                with sp.Fori(1, B // 2) as i2:
                    for u in range(2):
                        sp.wait_ge(prod_ready, i2 * (4 * JS) + (4 + 2 * (STEPS * g + JS * (u - 1))))
                        place_q(g, i2 * 2 + u, u)
            for i in range(at, len(WEIGHTS)):
                if i == PRE + RING_PRE:
                    sp.wait_ge(h_out, 2 * FC + 1)
                    for k in range(2):
                        sp.dma_start(brow[:, k, :], a[f"brow{k}"].partition_broadcast(P)).then_inc(brow_in, 16)
                load(i)
                if WEIGHTS[i] == "W1_0":
                    sp.wait_ge(xplus_ready, 1)
                    sp.dma_start(brow[:, 0, :], a["brow2"].partition_broadcast(P)).then_inc(brow_in, 16)
            for m in range(NM):
                sp.wait_ge(x_ready, NM * 3 + m + 1)
                sp.dma_start(out[m * P:(m + 1) * P, :], xrows[:, m, :]).then_inc(out_done, 16)
            sp.wait_ge(out_done, 16 * NM)

        @block.gpsimd
        def _(pool):
            pool.iota(iota_i, [[1, F]], base=0, channel_multiplier=0).then_inc(iota_made, 1)
            pool.memset(ident[:, :], 0.0).then_inc(const_made, 1)
            pool.memset(window[:, :], 0.0).then_inc(const_made, 1)
            pool.wait_ge(const_made, 2)
            pool.affine_select(out=ident[:, :], in_=ident[:, :], compare_op=ALU.not_equal, fill=1.0, base=0,
                               pattern=[[-1, P]], channel_multiplier=1).then_inc(const_made, 1)
            for n in range(NJ):
                pool.wait_ge(const_made, 3 + n)
                pool.memset(window[n * LH:(n + 1) * LH, P - NJ + n:P - NJ + n + 1], 1.0).then_inc(const_made, 1)
            pool.wait_ge(const_made, 7)
            pool.memset(ones_row[:, :], 1.0).then_inc(const_made, 1)
            pool.wait_ge(const_made, 8)
            pool.memset(epsc[:, :], EPS).then_inc(const_made, 1)
            wait_drained(pool, ("qg", 3, 1))
            for part, rows in ((0, qg_hi), (1, qg_lo)):
                for b2 in range(2):
                    for h in range(2):
                        p0 = (2 * b2 + h) * LH
                        dst = Mt[part * LH:(part + 1) * LH, b2:B:2, h, :].bitcast(F32)
                        pool.dma_start(dst, rows[p0:p0 + LH, :, :]).then_inc(qg_placed, 16)
            pool.sem_inc(halves_added, LAG)
            for g in range(2):
                for m in range(NM):
                    wait_drained(pool, ("hg", g, m, 1))
                    place_hg(pool, m, 1)
                for b in range(B):
                    for part in range(2):
                        pool.wait_ge(hg_in[part][b], 16 * (g + 1))
                    pool.sem_inc(hg_placed, 1)
                with pool.Fori(0, STEPS // ATT) as i:
                    for k in range(ATT):
                        pool.wait_ge(prod_ready, i * (2 * ATT) + (4 + 2 * (STEPS * g + k + 1)))
                        pool.tensor_tensor(att[:, k, 0, :], att[:, k, 0, :], att[:, k, 1, :], ALU.add).then_inc(
                            halves_added, 1)
            for k in range(3):
                pool.wait_ge(x_ready, NM * (k + 1))
                pool.wait_ge(brow_in, 16 * (2 if k < 2 else 3))
                if k == 2:
                    wait_drained(pool, ("Yr", 0, R - 1, NM - 1, 1))
                for m in range(NM):
                    ins = pool.tensor_tensor(xplus[k][m], xrows[:, m, :], brow[:, k % 2, :], ALU.add)
                    if m == NM - 1:
                        ins.then_inc(xplus_ready, 1)

        @block.tensor
        def _(pe):
            weight = [0]

            def next_weight(name):
                i = weight[0]
                assert WEIGHTS[i] == name, (WEIGHTS[i], name)
                pe.wait_ge(weight_in[weight_slot(i)], 16 * weight_uses(i))
                weight[0] += 1
                return wslot(i)

            def acquire(name):
                i = NUMBER[name]
                if i >= BANKS:
                    wait_drained(pe, TILES[i - BANKS][0])

            def rows_half(name, cols, w, m, h, extra=None):
                acquire(name)
                if extra is not None:
                    pe.matmul(psum(name, FH), extra[0], extra[1], start=True, stop=False)
                for c in range(FC):
                    mm = pe.matmul(psum(name, FH), cols(c, m), w[:, c, h * FH:(h + 1) * FH],
                                   start=(c == 0 and extra is None), stop=(c == FC - 1))
                mm.then_inc(tile_full, 1)
                return mm

            def cols_chunk(name, c, pairs):
                acquire(name)
                for k, (w, x) in enumerate(pairs):
                    mm = pe.matmul(psum(name, N), w[:, c * P:(c + 1) * P], x,
                                   start=(k == 0), stop=(k == len(pairs) - 1))
                mm.then_inc(tile_full, 1)

            def used():
                pe.drain().then_inc(weights_used, 1)

            def of(t):
                return lambda c, m: t[:, c, m * P:(m + 1) * P]

            def qk_weights(k):
                C = 2 * HEADS[k]
                acquire(("wqk", k))
                for r in range(R):
                    w = next_weight(f"W{k + 1}T_{r}")
                    for c in range(FC):
                        o = c * R * C + r * C
                        for f in range(FC):
                            mm = pe.matmul(psum(("wqk", k), 512)[:, o:o + C], w[:, f, c * P:(c + 1) * P],
                                           qk[k][:, f, :], start=(f == 0), stop=(f == FC - 1))
                    if r == R - 1:
                        mm.then_inc(tile_full, 1)
                    used()

            def edge_chunk(c, u, first, last):
                pe.wait_ge(hot_ready, c + 1)
                for m in range(NM):
                    for h in range(2):
                        mm = pe.matmul(psum(("A", m, h), FH), hot[u][:, F + m * P:F + (m + 1) * P],
                                       hot[u][:, h * FH:(h + 1) * FH], start=first, stop=last,
                                       skip_group_check=True)
                mm.then_inc(hot_used, 1)
                return mm

            for u in range(HOT):
                edge_chunk(u, u, u == 0, False)
            with pe.Fori(1, EC // HOT - 1) as i:
                for u in range(HOT):
                    edge_chunk(i * HOT + u, u, False, False)
            for u in range(HOT):
                edge_chunk(EC - HOT + u, u, False, u == HOT - 1)
            pe.drain().then_inc(tile_full, 4)

            pe.wait_ge(q_in, 32)
            pe.wait_ge(const_made, 9)
            pe.wait_ge(small_in, 16 * 4)
            w = next_weight("WgT_q")
            for c4 in range(4):
                for h in range(2):
                    rows_half(("qg", c4, h), lambda c, m: qT[c // 3][:, c % 3, m * P:(m + 1) * P], w, c4, h,
                              (ones_row[:, :], bg_row[:, h * FH:(h + 1) * FH]))
            used()

            pe.wait_ge(graph_ready, 1)
            for s in range(NM):
                for r in range(R):
                    acquire(("AnT", s, r))
                    for m in range(NM):
                        mm = pe.transpose(psum(("AnT", s, r), N)[:, m * P:(m + 1) * P],
                                          AnS[:, m, r, s * P:(s + 1) * P], ident[:, :])
                    mm.then_inc(tile_full, 1)
            pe.wait_ge(graph_ready, 2)
            for s in range(NM):
                acquire(("AgT", s))
                for m in range(NM):
                    mm = pe.transpose(psum(("AgT", s), N)[:, m * P:(m + 1) * P],
                                      AgS[:, m, s * P:(s + 1) * P], ident[:, :])
                mm.then_inc(tile_full, 1)

            pe.wait_ge(x_in, 16)
            for g in range(2):
                x = (XT, HB)[g]
                if g == 1:
                    pe.wait_ge(h_out, FC)
                for r in range(R):
                    w = next_weight(f"Wrel{g + 1}_{r}")
                    for m in range(NM):
                        for h in range(2):
                            rows_half(("Y", g, r, m, h), of(x), w, m, h)
                    used()
                w = next_weight(f"Wroot{g + 1}")
                wait_drained(pe, ("Y", g, R - 1, NM - 1, 0), ("Y", g, R - 1, NM - 1, 1))
                if g == 0:
                    wait_drained(pe, ("AnT", 1, 0), ("AnT", 1, 1), ("AnT", 1, 2))
                for c in range(FC):
                    cols_chunk(("agg", g, c), c, [(w[:, k, :], x[:, k, :]) for k in range(FC)]
                               + [(Y[:, s, r, :], AnT[:, s, r, :]) for r in range(R) for s in range(NM)])
                used()
                w = next_weight("WgT_h")
                wait_drained(pe, ("agg", g, FC - 1), ("agg", g, FC - 2))
                for m in range(NM):
                    for h in range(2):
                        rows_half(("hg", g, m, h), of(HA), w, m, h)
                used()

                qk_weights(g)
                def gate_sum(i, k):
                    if k % JS == 0:
                        pe.wait_ge(hg_placed, i * (B // NM) + (B * g + k // JS + 1))
                    for n in range(3):
                        if n < 2:
                            pe.wait_ge(prod_ready, i * STEPS + (2 * (STEPS * g + k) + 1 + n))
                        mm = pe.matmul(gsum[k % 2][:, n * 512:(n + 1) * 512], sel[:, k % JS, :],
                                       Mt_graph[:, bass.ds(i * (B // NM) + k // JS, 1), n * 512:(n + 1) * 512],
                                       start=True, stop=True)
                        if n != 1:
                            mm.then_inc(sum_ready, 1)

                def gate_reduce(k, added):
                    pe.wait_ge(halves_added, added)
                    z = P - NJ - k * NJ
                    for h in range(2):
                        mm = pe.matmul(gqi[h], window[:, z:z + P], att[:, k % ATT, 0, h * FH:(h + 1) * FH],
                                       start=(k == 0), stop=(k == STEPS // NM - 1), skip_group_check=True)
                    mm.then_inc(prods_summed, 1)

                wait_drained(pe, ("hg", g, NM - 1, 1), ("wqk", g))
                pe.wait_ge(sel_made, 4)
                if g == 0:
                    pe.wait_ge(qg_placed, 16 * 8)
                with pe.Fori(0, NM) as i:
                    for k in range(STEPS // NM):
                        gate_sum(i, k)
                        if k == LAG:
                            pe.wait_ge(qi_rows, i + NM * g)
                        gate_reduce((k - LAG) % (STEPS // NM), i * (STEPS // NM) + (STEPS * g + k + 1))
                for k in range(STEPS // NM - LAG, STEPS // NM):
                    gate_reduce(k, STEPS * g + STEPS // NM + k + 1 + LAG)
                pe.wait_ge(qi_rows, NM * (g + 1))
                for c in range(FC):
                    acquire(("qiT", g, c))
                    for m in range(NM):
                        mm = pe.transpose(psum(("qiT", g, c), N)[:, m * P:(m + 1) * P],
                                          yrows[:, m, c * P:(c + 1) * P], ident[:, :])
                    mm.then_inc(tile_full, 1)

                wh = next_weight("WqT_h")
                wq = next_weight("WqT_q")
                wait_drained(pe, ("qiT", g, FC - 2), ("qiT", g, FC - 1))
                for c in range(FC):
                    cols_chunk(("alpha", g, c), c, [(wh[:, k, :], HA[:, k, :]) for k in range(FC)]
                               + [(wq[:, k, :], qiT[:, k, :]) for k in range(FC)])
                used()
                used()

            pe.wait_ge(h_out, 2 * FC + 1)
            for m in range(NM):
                for h in range(2):
                    acquire(("back", m, h))
                    for c in range(3):
                        mm = pe.transpose(psum(("back", m, h), FH)[:, c * P:(c + 1) * P],
                                          HA[:, 3 * h + c, m * P:(m + 1) * P], ident[:, :])
                    mm.then_inc(tile_full, 1)

            def x_to_cols(k):
                pe.wait_ge(x_ready, NM * (k + 1))
                for c in range(FC):
                    acquire(("xT", k, c))
                    for m in range(NM):
                        mm = pe.transpose(psum(("xT", k, c), N)[:, m * P:(m + 1) * P],
                                          xrows[:, m, c * P:(c + 1) * P], ident[:, :])
                    mm.then_inc(tile_full, 1)
                wait_drained(pe, ("xT", k, FC - 1), ("xT", k, FC - 2))

            def gcn_product(k, name, x):
                w = next_weight(name)
                for m in range(NM):
                    for h in range(2):
                        rows_half(("Yg", k, m, h), of(x), w, m, h)
                used()
                wait_drained(pe, ("Yg", k, 1, 0), ("Yg", k, 1, 1))

            def gcn_rows(k, slot):
                for m in range(NM):
                    for h in range(2):
                        acquire(("out", k, m, h))
                        for s in range(NM):
                            mm = pe.matmul(psum(("out", k, m, h), FH), AgT[:, s, m * P:(m + 1) * P],
                                           Y[:, s, slot, h * FH:(h + 1) * FH], start=(s == 0), stop=(s == NM - 1))
                        mm.then_inc(tile_full, 1)

            x_to_cols(0)
            gcn_product(0, "gcn1", HB)
            wait_drained(pe, ("AgT", 1))
            for c in range(FC):
                cols_chunk(("agg", 2, c), c, [(Y[:, s, 0, :], AgT[:, s, :]) for s in range(NM)])
            wait_drained(pe, ("agg", 2, FC - 1), ("agg", 2, FC - 2))
            gcn_product(1, "gcn2", HA)
            gcn_rows(0, 1)
            x_to_cols(1)
            gcn_product(2, "gcn3", HB)
            gcn_rows(1, 0)
            x_to_cols(2)

            for k in range(2):
                H, C = HEADS[k], 2 * HEADS[k]
                x = (HB, HA)[k]
                if k == 1:
                    pe.wait_ge(h_out, 2 * FC + 2)
                wait_drained(pe, ("wqk", k))
                acquire(("QN", k))
                for m in range(NM):
                    for c in range(FC):
                        mm = pe.matmul(psum(("QN", k), 512)[:, m * R * C:(m + 1) * R * C], x[:, c, m * P:(m + 1) * P],
                                       wqk[k][:, c, :], start=(c == 0), stop=(c == FC - 1))
                mm.then_inc(tile_full, 1)
                acquire(("KT", k))
                for c in range(FC):
                    mm = pe.matmul(psum(("KT", k), N, R * C), wqk[k][:, c, :], x[:, c, :],
                                   start=(c == 0), stop=(c == FC - 1))
                mm.then_inc(tile_full, 1)
                wait_drained(pe, ("KT", k))
                for i in range((H * R + 1) // 2):
                    acquire(("Kb", k, i))
                    for e in range(2 * i, min(2 * i + 2, H * R)):
                        col = (e % R) * C + H + e // R
                        mm = pe.matmul(psum(("Kb", k, i), 512)[:, (e % 2) * N:(e % 2 + 1) * N],
                                       ident[0:R * C, col:col + 1].broadcast_to([R * C, P]), KT[0:R * C, :],
                                       start=True, stop=True)
                    mm.then_inc(tile_full, 1)
                for r in range(R):
                    w = next_weight(f"W{k + 1}_{r}")
                    for m in range(NM):
                        for h in range(2):
                            rows_half(("Yr", k, r, m, h), of(x), w, m, h)
                    used()
                for m in range(NM):
                    for h in range(H):
                        pe.wait_ge(p_ready, k * NM * HEADS[0] + m * H + h + 1)
                        for s in range(NM):
                            name = ("PT", k, m, h, s)
                            acquire(name)
                            for r in range(R):
                                mm = pe.transpose(psum(name, FH)[:, r * P:(r + 1) * P],
                                                  U[:, m, h, r, s * P:(s + 1) * P], ident[:, :])
                            mm.then_inc(tile_full, 1)
                wait_drained(pe, ("PT", k, NM - 1, H - 1, 0), ("PT", k, NM - 1, H - 1, 1),
                             ("Yr", k, R - 1, NM - 1, 1))
                for m in range(NM):
                    for h in range(2):
                        name = ("att", m, h) if k == 0 else ("out", 2, m, h)
                        acquire(name)
                        D = F // H if k == 0 else FH
                        for e in range(FH // D):
                            head = (2 * h + e) if k == 0 else 0
                            f0 = h * FH + e * D
                            for n in range(R * NM):
                                mm = pe.matmul(psum(name, FH)[:, e * D:(e + 1) * D],
                                               PT[:, n % NM, head, n // NM, m * P:(m + 1) * P],
                                               Y[:, n % NM, n // NM, f0:f0 + D],
                                               start=(n == 0), stop=(n == R * NM - 1))
                        mm.then_inc(tile_full, 1)
                if k == 0:
                    wait_drained(pe, ("att", NM - 1, 1))
                    for c in range(FC):
                        acquire(("hT", c))
                        for m in range(NM):
                            mm = pe.transpose(psum(("hT", c), N)[:, m * P:(m + 1) * P],
                                              yrows[:, m, c * P:(c + 1) * P], ident[:, :])
                        mm.then_inc(tile_full, 1)

        @block.scalar
        def _(act):
            def drain_copy(name, dst, src):
                wait_full(act, name)
                act.activation(dst, src, ACT.Copy).then_inc(drained["A"], 1)

            for m in range(NM):
                drain_copy(("A", m, 0), Acnt[:, m, :, :].rearrange("p r n -> p (r n)")[:, 0:FH], psum(("A", m, 0), FH))
            act.wait_ge(deg_ready, 1)
            act.activation(cnt[:, :, 7], cnt[:, :, 3], ACT.Sqrt).then_inc(root_ready, 1)
            for c in range(4):
                for h in range(2):
                    wait_full(act, ("qg", c, h))
                    act.activation(qg_hi[:, c, h * FH:(h + 1) * FH].bitcast(F32R), psum(("qg", c, h), FH),
                                   ACT.Copy).then_inc(qg_hi_ready, 1)
            for g in range(2):
                if g == 0:
                    for s in range(NM):
                        for r in (0, 2):
                            drain_copy(("AnT", s, r), AnT[:, s, r, :], psum(("AnT", s, r), N))
                for r in range(R):
                    for m in range(NM):
                        drain_copy(("Y", g, r, m, 0), Y[:, m, r, 0:FH], psum(("Y", g, r, m, 0), FH))
                if g == 0:
                    act.wait_ge(small_in, 16 * 4)
                for c in range(0, FC, 2):
                    wait_full(act, ("agg", g, c))
                    act.activation(HA[:, c, :], psum(("agg", g, c), N), ACT.Relu,
                                   bias=bcol[:, g, c:c + 1]).then_inc(drained["A"], 1)
                for m in range(NM):
                    for h in range(2):
                        wait_full(act, ("hg", g, m, h))
                        act.activation(hg_hi[m][:, h * FH:(h + 1) * FH].bitcast(F32R), psum(("hg", g, m, h), FH),
                                       ACT.Copy).then_inc(hg_hi_ready, 1)
                drain_copy(("wqk", g), wqk[g][:, :, :].rearrange("p c n -> p (c n)"),
                           psum(("wqk", g), FC * R * 2 * HEADS[g]))

                def sigmoids(first, end):
                    with act.Fori(first // 2, end // 2) as i:
                        for k in range(2):
                            for n in range(2):
                                act.wait_ge(sum_ready, i * 4 + (2 * STEPS * g + 2 * k + n + 1))
                                v = gsum[k][:, CHUNKS[n]]
                                act.activation(v, v, ACT.Sigmoid).then_inc(sig_ready, 1)

                def drain_qi(m):
                    act.wait_ge(prods_summed, REDS * g + LAG + STEPS // NM * (m + 1))
                    for h in range(2):
                        ins = act.activation(yrows[:, m, h * FH:(h + 1) * FH], gqi[h], ACT.Copy)
                    ins.then_inc(qi_rows, 1)

                half = STEPS // NM + LAG + 1
                sigmoids(0, half)
                drain_qi(0)
                sigmoids(half, STEPS)
                drain_qi(1)
                for c in range(0, FC, 2):
                    drain_copy(("qiT", g, c), qiT[:, c, :], psum(("qiT", g, c), N))
                wait_drained(act, ("qiT", g, FC - 2), ("qiT", g, FC - 1))
                act.activation(TY[:, :], QX[:, :], ACT.Tanh).then_inc(tanh_ready, 1)
                for c in range(FC):
                    wait_full(act, ("alpha", g, c))
                    act.activation(alpha[:, c, :], psum(("alpha", g, c), N), ACT.Sigmoid,
                                   bias=bcol[:, 2, c:c + 1]).then_inc(drained["A"], 1)

            def layer_norm_std(k):
                for m in range(NM):
                    act.wait_ge(var_ready, NM * k + m + 1)
                    act.activation(mv[:, m, 2:3], mv[:, m, 1:2], ACT.Sqrt, bias=epsc[:, :]).then_inc(std_ready, 1)

            def drain_x(k):
                for c in range(0, FC, 2):
                    drain_copy(("xT", k, c), HB[:, c, :], psum(("xT", k, c), N))

            def drain_gcn(k, slot):
                for m in range(NM):
                    drain_copy(("Yg", k, m, 0), Y[:, m, slot, 0:FH], psum(("Yg", k, m, 0), FH))

            act.wait_ge(const_made, 9)
            layer_norm_std(0)
            drain_x(0)
            drain_gcn(0, 0)
            for c in range(0, FC, 2):
                wait_full(act, ("agg", 2, c))
                act.activation(HA[:, c, :], psum(("agg", 2, c), N), ACT.Relu,
                               bias=bcol[:, 3, c:c + 1]).then_inc(drained["A"], 1)
            drain_gcn(1, 1)
            layer_norm_std(1)
            drain_x(1)
            drain_gcn(2, 0)
            layer_norm_std(2)
            drain_x(2)
            for k in range(2):
                H, C = HEADS[k], 2 * HEADS[k]
                drain_copy(("QN", k), QN[:, :, 0:R * C], psum(("QN", k), NM * R * C).rearrange("p (m c) -> p m c", m=NM))
                drain_copy(("KT", k), KT[0:R * C, :], psum(("KT", k), N, R * C))
                wait_drained(act, ("KT", k))
                for i in range((H * R + 1) // 2):
                    wait_full(act, ("Kb", k, i))
                    for e in range(2 * i, min(2 * i + 2, H * R)):
                        h, r = e // R, e % R
                        for m in range(NM):
                            ins = act.activation(U[:, m, h, r, :], psum(("Kb", k, i), 512)[:, (e % 2) * N:(e % 2 + 1) * N],
                                                 ACT.Identity, bias=QN[:, m, r * C + h:r * C + h + 1])
                    ins.then_inc(drained["A"], 1)

                def exps(m):
                    act.wait_ge(nmax_ready, NM * k + m + 1)
                    for h in range(H):
                        v = U[:, m, h, :, :].rearrange("p r n -> p (r n)")
                        act.activation(v, v, ACT.Exp, bias=smx[:, m, 1, h:h + 1]).then_inc(e_ready, 1)

                for r in range(R):
                    for m in range(NM):
                        for h in range(2):
                            drain_copy(("Yr", k, r, m, h), Y[:, m, r, h * FH:(h + 1) * FH], psum(("Yr", k, r, m, h), FH))
                    if r < NM:
                        exps(r)
                for m in range(NM):
                    for h in range(H):
                        drain_copy(("PT", k, m, h, 0), PT[:, 0, h, :, m * P:(m + 1) * P],
                                   psum(("PT", k, m, h, 0), FH).rearrange("p (r n) -> p r n", r=R))
                if k == 0:
                    for c in range(FC):
                        wait_full(act, ("hT", c))
                        act.activation(HA[:, c, :], psum(("hT", c), N), ACT.Identity,
                                       bias=bcol[:, 4, c:c + 1]).then_inc(drained["A"], 1)
                    act.wait_ge(elu_min, 1)
                    act.activation(elu_m, elu_m, ACT.Exp).then_inc(elu_exp, 1)
            layer_norm_std(3)

        @block.vector
        def _(dve):
            links = [0]

            def link(ins):
                links[0] += 1
                ins.then_inc(dve_chain, 1)
                dve.wait_ge(dve_chain, links[0])

            def drain_copy(name, dst, src):
                wait_full(dve, name)
                dve.tensor_copy(dst, src).then_inc(drained["V"], 1)

            dve.sem_inc(prod_ready, 4)
            dve.wait_ge(ints_in, 48)
            dve.wait_ge(iota_made, 1)
            dve.tensor_copy(iota_h, iota_i)
            link(dve.tensor_copy(idxf[:, :, :], idx[:, :, :]))
            link(dve.scalar_tensor_tensor(out=comb[:, :], in0=idxf[:, 2, :], scalar=float(N), in1=idxf[:, 1, :],
                                          op0=ALU.mult, op1=ALU.add))

            def one_hots(c, u, wait):
                if wait:
                    dve.wait_ge(hot_used, c - (HOT - 1))
                dve.tensor_scalar(hot[u][:, 0:F], iota_h, comb[:, bass.ds(c, 1)], None, ALU.is_equal)
                dve.tensor_scalar(hot[u][:, F:F + N], iota_h[:, 0:N], idxf[:, 0, bass.ds(c, 1)], None,
                                  ALU.is_equal).then_inc(hot_ready, 1)

            for u in range(HOT):
                one_hots(u, u, False)
            with dve.Fori(1, EC // HOT) as i:
                for u in range(HOT):
                    one_hots(i * HOT + u, u, True)

            dve.wait_ge(const_made, 9)
            v = sel[:, :, :].rearrange("p j (n l) -> p j n l", n=NJ)
            for part in range(2):
                p0 = part * LH
                dve.tensor_copy(v[p0:p0 + LH], ident[p0:p0 + LH, p0:p0 + LH].unsqueeze(1).unsqueeze(1).broadcast_to(
                    [LH, JS, NJ, LH])).then_inc(sel_made, 1)
                p0 = (2 + part) * LH
                dve.tensor_copy(sel[p0:p0 + LH, :, :].rearrange("p j (n l) -> p (j n) l", n=NJ),
                                ident[p0:p0 + LH, p0:p0 + LH].unsqueeze(2).broadcast_to([LH, NB, LH])).then_inc(
                    sel_made, 1)

            for m in range(NM):
                drain_copy(("A", m, 1), Acnt[:, m, :, :].rearrange("p r n -> p (r n)")[:, FH:F], psum(("A", m, 1), FH))
            wait_drained(dve, ("A", 1, 0), ("A", 1, 1))
            link(dve.tensor_reduce(cnt[:, :, 0:R], Acnt[:, :, :, :], AX.X, ALU.add))
            link(dve.tensor_reduce(cnt[:, :, 3:4], cnt[:, :, 0:R], AX.X, ALU.add))
            dve.tensor_scalar(cnt[:, :, 3:4], cnt[:, :, 3:4], 1.0, None, ALU.add).then_inc(deg_ready, 1)
            link(dve.tensor_scalar(cnt[:, :, 4:7], cnt[:, :, 0:R], 1.0, None, ALU.max))
            link(dve.reciprocal(cnt[:, :, 4:7], cnt[:, :, 4:7]))
            for m in range(NM):
                for r in range(R):
                    ins = dve.tensor_scalar(AnS[:, m, r, :], Acnt[:, m, r, :], cnt[:, m, 4 + r:5 + r], None, ALU.mult)
            ins.then_inc(graph_ready, 1)
            link(dve.tensor_tensor(AgS, Acnt[:, :, 0, :], Acnt[:, :, 1, :], ALU.add))
            link(dve.tensor_tensor(AgS, AgS, Acnt[:, :, 2, :], ALU.add))
            for m in range(NM):
                d = AgS[:, m, m * P:(m + 1) * P]
                link(dve.tensor_tensor(d, d, ident[:, :], ALU.add))
            dve.wait_ge(root_ready, 1)
            link(dve.reciprocal(cnt[:, :, 7], cnt[:, :, 7]))
            for m in range(NM):
                ins = dve.tensor_scalar(AgS[:, m, :], AgS[:, m, :], cnt[:, m, 7:8], None, ALU.mult)
            ins.then_inc(graph_ready, 1)

            for c in range(4):
                for h in range(2):
                    dve.wait_ge(qg_hi_ready, 2 * c + h + 1)
                    f = slice(h * FH, (h + 1) * FH)
                    dve.tensor_tensor(qg_lo[:, c, f].bitcast(F32R), psum(("qg", c, h), FH), qg_hi[:, c, f],
                                      ALU.subtract).then_inc(drained["V"], 1)
            for g in range(2):
                if g == 0:
                    for s in range(NM):
                        drain_copy(("AnT", s, 1), AnT[:, s, 1, :], psum(("AnT", s, 1), N))
                    for s in range(NM):
                        wait_full(dve, ("AgT", s))
                        dve.tensor_scalar(AgT[:, s, :], psum(("AgT", s), N), cnt[:, s, 7:8], None, ALU.mult).then_inc(
                            drained["V"], 1)
                for r in range(R):
                    for m in range(NM):
                        drain_copy(("Y", g, r, m, 1), Y[:, m, r, FH:F], psum(("Y", g, r, m, 1), FH))
                if g == 0:
                    dve.wait_ge(small_in, 16 * 4)
                for c in range(1, FC, 2):
                    wait_full(dve, ("agg", g, c))
                    dve.tensor_scalar(HA[:, c, :], psum(("agg", g, c), N), bcol[:, g, c:c + 1], 0.0, ALU.add,
                                      ALU.max).then_inc(drained["V"], 1)
                for m in range(NM):
                    for h in range(2):
                        dve.wait_ge(hg_hi_ready, 4 * g + 2 * m + h + 1)
                        f = slice(h * FH, (h + 1) * FH)
                        dve.tensor_tensor(hg_lo[m][:, f].bitcast(F32R), psum(("hg", g, m, h), FH), hg_hi[m][:, f],
                                          ALU.subtract).then_inc(drained["V"], 1)

                with dve.Fori(0, B // 2) as i2:
                    for k in range(2 * JS):
                        u = k // JS
                        if k % JS == 0:
                            dve.wait_ge(qrep_in[u], i2 * (16 * NJ) + 16 * NJ * (B // 2 * g + 1))
                        dve.wait_ge(prods_summed, i2 * (2 * JS) + (REDS * g + k))
                        for n in range(2):
                            dve.wait_ge(sig_ready, i2 * (4 * JS) + (2 * (STEPS * g + k) + n + 1))
                            dve.tensor_tensor(att_flat[k % ATT][:, CHUNKS[n]], gsum[k % 2][:, CHUNKS[n]],
                                              qrep_flat[u][:, CHUNKS[n]], ALU.mult).then_inc(prod_ready, 1)
                for c in range(1, FC, 2):
                    drain_copy(("qiT", g, c), qiT[:, c, :], psum(("qiT", g, c), N))
                dve.wait_ge(tanh_ready, g + 1)
                link(dve.tensor_tensor(thT, thT, HA[:, :, :], ALU.subtract))
                for c in range(FC):
                    wait_drained(dve, ("alpha", g, c))
                    link(dve.tensor_tensor(alpha[:, c, :], alpha[:, c, :], thT[:, c, :], ALU.mult))
                    dve.tensor_tensor(HB[:, c, :], alpha[:, c, :], HA[:, c, :], ALU.add).then_inc(h_out, 1)
            dve.wait_ge(h_out, 2 * FC)
            dve.tensor_tensor(HA[:, :, :], HB[:, :, :], XT[:, :, :], ALU.add).then_inc(h_out, 1)

            def layer_norm(k, source, drains):
                for m in range(NM):
                    for h in range(2):
                        if drains:
                            wait_full(dve, ("back", m, h))
                        link(dve.bn_stats(stat[:, m, h, :], source(m, h)))
                    dve.bn_aggr(mv[:, m, 0:2], stat[:, m, :, :]).then_inc(var_ready, 1)
                for m in range(NM):
                    dve.wait_ge(std_ready, NM * k + m + 1)
                    link(dve.reciprocal(mv[:, m, 3:4], mv[:, m, 2:3]))
                    for h in range(2):
                        ins = dve.tensor_scalar(xrows[:, m, h * FH:(h + 1) * FH], source(m, h), mv[:, m, 0:1],
                                                mv[:, m, 3:4], ALU.subtract, ALU.mult)
                        if drains:
                            ins.then_inc(drained["V"], 1)
                    if drains:
                        dve.wait_ge(drained["V"], DRAINS[("back", m, 1)])
                        dve.drain().then_inc(x_ready, 1)
                    else:
                        ins.then_inc(x_ready, 1)

            def y_half(m, h):
                return yrows[:, m, h * FH:(h + 1) * FH]

            def drain_x(k):
                for c in range(1, FC, 2):
                    drain_copy(("xT", k, c), HB[:, c, :], psum(("xT", k, c), N))

            def drain_gcn(k, slot):
                for m in range(NM):
                    drain_copy(("Yg", k, m, 1), Y[:, m, slot, FH:F], psum(("Yg", k, m, 1), FH))

            def residual(k):
                dve.wait_ge(xplus_ready, k + 1)
                for m in range(NM):
                    for h in range(2):
                        wait_full(dve, ("out", k, m, h))
                        dve.tensor_tensor(y_half(m, h), psum(("out", k, m, h), FH), xplus[k][m][:, h * FH:(h + 1) * FH],
                                          ALU.add).then_inc(drained["V"], 1)
                wait_drained(dve, ("out", k, 1, 1))

            layer_norm(0, lambda m, h: psum(("back", m, h), FH), True)
            drain_x(0)
            dve.tensor_scalar(hide[:, :, :, :], Acnt[:, :, :, :], 0.0, -BIG, ALU.is_equal, ALU.mult)
            drain_gcn(0, 0)
            for c in range(1, FC, 2):
                wait_full(dve, ("agg", 2, c))
                dve.tensor_scalar(HA[:, c, :], psum(("agg", 2, c), N), bcol[:, 3, c:c + 1], 0.0, ALU.add,
                                  ALU.max).then_inc(drained["V"], 1)
            drain_gcn(1, 1)
            residual(0)
            layer_norm(1, y_half, False)
            drain_x(1)
            drain_gcn(2, 0)
            residual(1)
            layer_norm(2, y_half, False)
            drain_x(2)
            for k in range(2):
                H, C = HEADS[k], 2 * HEADS[k]
                wait_drained(dve, ("Kb", k, (H * R + 1) // 2 - 1))
                for m in range(NM):
                    v = U[:, m, 0:H, :, :].rearrange("p h r n -> p (h r n)")
                    link(dve.scalar_tensor_tensor(out=v, in0=v, scalar=SLOPE, in1=v, op0=ALU.mult, op1=ALU.max))
                    for h in range(H):
                        v = U[:, m, h, :, :].rearrange("p r n -> p (r n)")
                        ins = dve.tensor_tensor_reduce(v, v, hide[:, m, :, :].rearrange("p r n -> p (r n)"), 1.0,
                                                       -3e38, ALU.add, ALU.max, smx[:, m, 0, h:h + 1])
                    link(ins)
                    dve.tensor_scalar(smx[:, m, 1, 0:H], smx[:, m, 0, 0:H], -1.0, None, ALU.mult).then_inc(nmax_ready, 1)
                for m in range(NM):
                    for h in range(H):
                        dve.wait_ge(e_ready, k * NM * HEADS[0] + m * H + h + 1)
                        v = U[:, m, h, :, :].rearrange("p r n -> p (r n)")
                        ins = dve.tensor_tensor_reduce(v, v, Acnt[:, m, :, :].rearrange("p r n -> p (r n)"), 1.0,
                                                       0.0, ALU.mult, ALU.add, smx[:, m, 2, h:h + 1])
                        ins.then_inc(p_ready, 1)
                    dve.wait_ge(p_ready, k * NM * HEADS[0] + (m + 1) * H)
                    link(dve.tensor_scalar(smx[:, m, 3, 0:H], smx[:, m, 2, 0:H], EPS_Z, None, ALU.add))
                    link(dve.reciprocal(smx[:, m, 3, 0:H], smx[:, m, 3, 0:H]))
                for m in range(NM):
                    for h in range(H):
                        drain_copy(("PT", k, m, h, 1), PT[:, 1, h, :, m * P:(m + 1) * P],
                                   psum(("PT", k, m, h, 1), FH).rearrange("p (r n) -> p r n", r=R))
                if k == 0:
                    D = F // H
                    for m in range(NM):
                        for h in range(2):
                            wait_full(dve, ("att", m, h))
                            for e in range(2):
                                head = 2 * h + e
                                ins = dve.tensor_scalar(yrows[:, m, head * D:(head + 1) * D],
                                                        psum(("att", m, h), FH)[:, e * D:(e + 1) * D],
                                                        smx[:, m, 3, head:head + 1], None, ALU.mult)
                            ins.then_inc(drained["V"], 1)
                    wait_drained(dve, ("hT", FC - 1))
                    t = flat(HA)
                    dve.tensor_scalar(elu_m, t, 0.0, None, ALU.min).then_inc(elu_min, 1)
                    dve.wait_ge(elu_min, 1)
                    link(dve.tensor_scalar(t, t, 0.0, -1.0, ALU.max, ALU.add))
                    dve.wait_ge(elu_exp, 1)
                    dve.tensor_tensor(t, t, elu_m, ALU.add).then_inc(h_out, 1)
                else:
                    dve.wait_ge(xplus_ready, 3)
                    for m in range(NM):
                        for h in range(2):
                            wait_full(dve, ("out", 2, m, h))
                            dve.scalar_tensor_tensor(out=y_half(m, h), in0=psum(("out", 2, m, h), FH),
                                                     scalar=smx[:, m, 3, 0:1],
                                                     in1=xplus[2][m][:, h * FH:(h + 1) * FH],
                                                     op0=ALU.mult, op1=ALU.add).then_inc(drained["V"], 1)
                    wait_drained(dve, ("out", 2, 1, 1))
            layer_norm(3, y_half, False)


def kernel(**inputs):
    import numpy as np
    import concourse.bacc as bacc
    from concourse import mybir as mb
    from concourse.bass_utils import run_bass_kernel_spmd as run

    def cols(w):
        return np.ascontiguousarray(np.transpose(w))

    def chunks(v):
        return np.ascontiguousarray(np.swapaxes(v.reshape(FC, P, -1), 0, 1))

    v = {k: np.asarray(x) for k, x in inputs.items()}
    q = v["L0_gnn_query_embs"].reshape(B * L, F)
    arrays = {
        "dst": v["dst"], "src": v["src"], "etype": v["edge_type_3"],
        "xT": cols(v["x"]), "q": q, "qT": cols(q), "bg": v["L0_gnn_bg"].reshape(1, F),
        "bias_cols": np.ascontiguousarray(np.stack([v[n].reshape(FC, P).T for n in (
            "L0_gnn_b1", "L0_gnn_b2", "L0_gnn_bq", "L1_gnn_b1", "L3_gnn_b1")], axis=1)),
        "brow0": v["L1_gnn_b2"], "brow1": v["L2_gnn_b"], "brow2": v["L3_gnn_b2"],
        "qk0": chunks(np.concatenate([v["L3_gnn_q1"], v["L3_gnn_k1"]], axis=1)),
        "qk1": chunks(np.concatenate([v["L3_gnn_q2"], v["L3_gnn_k2"]], axis=1)),
        "WgT_h": cols(v["L0_gnn_Wg"][:, :F]), "WgT_q": cols(v["L0_gnn_Wg"][:, F:]),
        "WqT_h": cols(v["L0_gnn_Wq"][:, :F]), "WqT_q": cols(v["L0_gnn_Wq"][:, F:]),
        "Wroot1": v["L0_gnn_W_root1"], "Wroot2": v["L0_gnn_W_root2"],
        "gcn1": v["L1_gnn_W1"], "gcn2": v["L1_gnn_W2"], "gcn3": v["L2_gnn_W"],
    }
    for r in range(R):
        arrays[f"Wrel1_{r}"] = v["L0_gnn_W_rel1"][r]
        arrays[f"Wrel2_{r}"] = v["L0_gnn_W_rel2"][r]
        arrays[f"W1_{r}"], arrays[f"W1T_{r}"] = v["L3_gnn_W1"][r], cols(v["L3_gnn_W1"][r])
        arrays[f"W2_{r}"], arrays[f"W2T_{r}"] = v["L3_gnn_W2"][r], cols(v["L3_gnn_W2"][r])
    arrays = {k: np.ascontiguousarray(x) for k, x in arrays.items()}
    nc = bacc.Bacc("TRN2", target_bir_lowering=False, num_devices=1)
    a = {k: nc.dram_tensor(f"in_{k}", x.shape, mb.dt.from_np(x.dtype), kind="ExternalInput").ap()
         for k, x in arrays.items()}
    out = nc.dram_tensor("out_x", (N, F), mb.dt.float32, kind="ExternalOutput").ap()
    build(nc, a, out)
    r = run(nc, [{f"in_{k}": x for k, x in arrays.items()}], core_ids=[0])
    return r.results[0]["out_x"]
```

```python
from contextlib import ExitStack

import concourse.bass as bass
from concourse import mybir

P = 128
N = 256
NM = N // P
F = 768
FC = F // P
FH = F // 2
E = 4096
EC = E // P
R = 3
B = 8
NB = N // B
L = 64
LH = 32
NJ = 4
JS = NB // NJ
STEPS = B * JS
HEADS = (4, 1)
BANKS = 8
RING = 7
HOT = 4
ATT = 4
LAG = 3
CHUNKS = (slice(0, 512), slice(512, 2 * F))
REDS = STEPS + LAG
BIG = 1e30
EPS = 1e-5
EPS_Z = 1e-16
SLOPE = 0.2

ALU = mybir.AluOpType
ACT = mybir.ActivationFunctionType
AX = mybir.AxisListType
F32 = mybir.dt.float32
F32R = mybir.dt.float32r
F16 = mybir.dt.float16
BF16 = mybir.dt.bfloat16
I32 = mybir.dt.int32

WEIGHTS = ["WgT_q"]
GATE_AT = []
for _g in range(2):
    for _r in range(R):
        WEIGHTS += [f"W{_g + 1}T_{_r}", f"Wrel{_g + 1}_{_r}"][_r == R - 1:]
    WEIGHTS += [f"Wroot{_g + 1}", "WgT_h", f"W{_g + 1}T_{R - 1}"]
    GATE_AT.append(len(WEIGHTS))
    WEIGHTS += ["WqT_h", "WqT_q"]
WEIGHTS += ["gcn1", "gcn2", "gcn3"] + [f"W1_{_r}" for _r in range(R)] + [f"W2_{_r}" for _r in range(R)]
BY_POOL = [WEIGHTS.index(_n) for _n in ("WgT_q", "W1_1", "W1_2", "W2_0")]


def plan_tiles():
    t = [(("A", m, h), "AV"[h]) for m in range(NM) for h in range(2)]
    t += [(("qg", c, h), "S") for c in range(4) for h in range(2)]
    for g in range(2):
        for r in range(R):
            if r < R - 1:
                t += [(("wq", g, r, h), "AV"[h]) for h in range(2)]
            if (g, r) == (0, 0):
                t += [(("AnT", s, k), "S") for s in range(NM) for k in range(R)]
                t += [(("AgT", s), "V") for s in range(NM)]
            t += [(("Y", g, r, m, h), "S") for m in range(NM) for h in range(2)]
        t += [(("agg", g, c), "A") for c in range(FC)]
        t += [(("hg", g, m, h), "S") for m in range(NM) for h in range(2)]
        t += [(("wq", g, R - 1, h), "AV"[h]) for h in range(2)]
        t += [(("wqk", g), "S")]
        t += [(("qiT", g, c), "S") for c in range(FC)]
        t += [(("alpha", g, c), "A") for c in range(FC)]
    t += [(("out", 0, m, h), "V") for h in range(2) for m in range(NM)]
    t += [(("xT", 0, c), "S") for c in range(FC)]
    t += [(("Yg", 0, m, h), "S") for m in range(NM) for h in range(2)]
    t += [(("agg", 2, c), "A") for c in range(FC)]
    t += [(("Yg", 1, m, h), "S") for m in range(NM) for h in range(2)]
    t += [(("out", 1, m, h), "V") for m in range(NM) for h in range(2)]
    t += [(("xT", 1, c), "S") for c in range(FC)]
    t += [(("Yg", 2, m, h), "S") for m in range(NM) for h in range(2)]
    t += [(("out", 2, m, h), "V") for m in range(NM) for h in range(2)]
    t += [(("xT", 2, c), "S") for c in range(FC)]
    for k in range(2):
        t += [(("KT", k), "S"), (("QN", k), "A")]
        t += [(("Kb", k, i), "V") for i in range((HEADS[k] * R + 1) // 2)]
        t += [(("Yr", k, r, m, h), "AS"[k]) for r in range(R) for m in range(NM) for h in range(2)]
        t += [(("PT", k, m, h, s), "S" if k else "AV"[s]) for m in range(NM) for h in range(HEADS[k]) for s in range(NM)]
        if k == 0:
            t += [(("att", m, h), "V") for m in range(NM) for h in range(2)]
            t += [(("hT", c), "S") for c in range(FC)]
        else:
            t += [(("out", 3, m, h), "V") for m in range(NM) for h in range(2)]
    return t


TILES = plan_tiles()
NUMBER = {name: i for i, (name, _) in enumerate(TILES)}
KIND = dict(TILES)
DRAINS = {name: sum((e == "A") == (KIND[name] == "A") for _, e in TILES[:i + 1]) for name, i in NUMBER.items()}
HIGHS = {name: sum(e == "S" for _, e in TILES[:i + 1]) for name, i in NUMBER.items()}


def build(nc, a, result):
    ctx = ExitStack()
    with ctx:
        def sem(name):
            return ctx.enter_context(nc.semaphore(name))

        def sb(name, shape, dt=F32, stack=ctx):
            return stack.enter_context(nc.sbuf_tensor(name, shape, dt))

        Wh = sb("weight_high", [P, RING, F], F32R)
        with ExitStack() as stage:
            raw = sb("weight_raw", [P, RING, F], F32, stage)
        Wl = sb("weight_low", [P, RING, F], F32R)
        HA = sb("colsA", [P, 2, FC, N], F32R)
        HB = sb("colsB", [P, 2, FC, N], F32R)
        QX = sb("qi_cols", [P, 2, FC, N], F32R)
        TY = sb("y_rows", [P, NM, F])
        Hf = sb("h_cols", [P, FC, N])
        Acnt = sb("edge_counts", [P, NM, R, N])
        AnT = sb("mean_weights_T", [P, 2, NM, R, N], F32R)
        AgT = sb("gcn_weights_T", [P, 2, NM, N], F32R)
        ident = sb("ident", [P, P])
        sel = sb("gate_select", [P, JS, P], F32R)
        window = sb("ones_window", [P, 2 * P])
        bcol = sb("bias_cols", [P, 4, FC])
        qk = [sb(f"qk{k}", [P, FC, 2 * HEADS[k]]) for k in range(2)]
        qks = [sb(f"qk_split{k}", [P, FC, 2, 2 * HEADS[k]], F32R) for k in range(2)]
        fold = [sb(f"fold{k}", [4 * HEADS[k], 2 * HEADS[k]]) for k in range(2)]
        wqk = [sb(f"wqk{k}", [P, 2, FC, R * 2 * HEADS[k]], F32R) for k in range(2)]
        QN = sb("q_of_node", [P, NM, R * 2 * HEADS[0]])
        idxf = sb("edge_floats", [P, 3, EC])
        comb = sb("edge_rel_src", [P, EC])
        cnt = sb("counts", [P, NM, 8])
        stat = sb("bn_stats", [P, NM, 2, 6])
        mv = sb("mean_var", [P, NM, 4])
        smx = sb("softmax_small", [P, NM, 4, HEADS[0]])
        epsc = sb("eps", [P, 1])
        scratch = sb("scratch", [P, 1])

        with ExitStack() as stage:
            Mt = sb("gate_moving", [P, B, 2, F], F32R, stage)
            qrep = sb("q_replicated", [P, 2, 2, F], F32, stage)
            att = sb("gate_products", [P, ATT, 2, F], F32, stage)
        with ExitStack() as stage:
            x_raw = sb("x_raw", [P, FC, N], F32, stage)
            iota_i = sb("iota_i", [P, F], I32, stage)
            iota_h = sb("iota_h", [P, F], F16, stage)
            AnS = sb("mean_weights", [P, NM, R, N], F32, stage)
            AgS = sb("gcn_weights", [P, NM, N], F32, stage)
            hot_rows = sb("one_hots", [P, HOT, F + N], BF16, stage)
            idx = sb("edge_ints", [P, 3, EC], I32, stage)
            bg_raw = sb("bg_raw", [1, F], F32, stage)
            bg = sb("bg_split", [1, 2, F], F32R, stage)
            ones = sb("ones", [1, P], F32R, stage)
        with ExitStack() as stage:
            sb("moving_stays_0", [P, B, 2, F], F32R, stage)
            q_raw = sb("q_raw", [P, FC, 4 * P], F32, stage)
            qg = sb("qg_rows", [P, 2, 4, F], F32R, stage)
        with ExitStack() as stage:
            sb("moving_stays_1", [P, B, 2, F], F32R, stage)
            Y = sb("products", [P, 2, NM, R, F], F32R, stage)
        with ExitStack() as stage:
            U = sb("edge_scores", [P, NM, HEADS[0], R, N], F32, stage)
            PT = sb("edge_weights_T", [P, NM, HEADS[0], R, N], F32, stage)
            Yf = sb("rgat_products", [P, NM, R, F], F32, stage)
            xplus = sb("x_plus_bias", [P, NM, F], F32, stage)
            brow = sb("bias_rows", [P, 2, F], F32, stage)
            xrows = sb("x_rows", [P, NM, F], F32, stage)
        with ExitStack() as stage:
            U1 = sb("edge_scores_1", [P, NM, 1, R, N], F32, stage)
            PTs = sb("edge_weights_T_split", [P, 2, NM, R, N], F32R, stage)
            Ys = sb("rgat_products_split", [P, 2, NM, R, F], F32R, stage)
        with ExitStack() as stage:
            Yg = sb("gcn_products", [P, 2, 2, NM, F], F32R, stage)

        hot = [hot_rows[:, i, :] for i in range(HOT)]
        qT = [t[:, :, :, :].rearrange("p a c n -> p (a c n)").rearrange("p (c l) -> p c l", c=FC) for t in (HA, QX)]
        hg = HB[:, :, :, :].rearrange("p a c n -> p a (c n)").rearrange("p a (m f) -> p a m f", m=NM)
        alpha = att[:, 0, :, :].rearrange("p h f -> p (h f)").rearrange("p (c n) -> p c n", c=FC)
        thT = att[:, 1, :, :].rearrange("p h f -> p (h f)").rearrange("p (c n) -> p c n", c=FC)
        wq_rows = [TY[:, 0, :], TY[:, 1, :], att[:, 0, 1, :]]
        yrows = TY
        hide = AnT[:, 0]
        scores = [U, U1]
        KT = sel[0:R * 2 * HEADS[0], 0:4, :].rearrange("p j n -> p (j n)").rearrange("p (a n) -> p a n", a=2)
        ones_at = sel[0:R * 2 * HEADS[0], 4, 0:R * 2 * HEADS[0]]
        elu_m = U[:, 0, 0:2, :, :].rearrange("p h r n -> p (h r n)").rearrange("p (m f) -> p m f", m=NM)
        att_flat = [att[:, i, :, :].rearrange("p h f -> p (h f)") for i in range(ATT)]
        qrep_flat = [qrep[:, u, :, :].rearrange("p h f -> p (h f)") for u in range(2)]
        Mt_graph = Mt[:, :, :, :].rearrange("p b h f -> p b (h f)")

        ps = ctx.enter_context(nc.psum_tensor("ps", [P, BANKS, 512], F32))
        gsum = [ps[:, 3 * i:3 * i + 3, :].rearrange("p b n -> p (b n)") for i in range(2)]
        gqi = [ps[:, 6 + h, 0:FH] for h in range(2)]

        def psum(name, width, parts=P):
            return ps[0:parts, NUMBER[name] % BANKS, 0:width]

        tile_full = sem("tile_full")
        drained = {"A": sem("drained_by_act"), "V": sem("drained_by_dve")}
        raw_in = [sem(f"raw_in{s}") for s in range(RING)]
        high_made = sem("high_made")
        low_by_pool = sem("low_by_pool")
        low_by_dve = sem("low_by_dve")
        chunks_used = sem("chunks_used")
        tile_high = sem("tile_high")
        ints_in = sem("ints_in")
        x_in = sem("x_in")
        q_in = sem("q_in")
        small_in = sem("small_in")
        const_made = sem("const_made")
        iota_made = sem("iota_made")
        sel_made = sem("sel_made")
        hot_ready = sem("hot_ready")
        hot_used = sem("hot_used")
        deg_ready = sem("deg_ready")
        root_ready = sem("root_ready")
        graph_ready = sem("graph_ready")
        qg_placed = sem("qg_placed")
        hg_in = [sem(f"hg_in{b}") for b in range(B)]
        hg_placed = sem("hg_placed")
        qrep_in = [sem(f"qrep_in{u}") for u in range(2)]
        att_clean = sem("att_clean")
        sum_ready = sem("sum_ready")
        sig_ready = sem("sig_ready")
        prod_ready = sem("prod_ready")
        halves_added = sem("halves_added")
        prods_summed = sem("prods_summed")
        qi_rows = sem("qi_rows")
        tanh_ready = sem("tanh_ready")
        bg_high = sem("bg_high")
        bg_split = sem("bg_split")
        q_high = sem("q_high")
        x_high = sem("x_high")
        q_split = sem("q_split")
        x_split = sem("x_split")
        qk_split = sem("qk_split")
        cols_out = sem("cols_out")
        AFTER = {"h0": 0, "gate0": FC, "h1": 2 * FC, "gcn": 3 * FC}
        th_ready = sem("th_ready")
        gate_scaled = sem("gate_scaled")
        gate_added = sem("gate_added")
        x_rows_in = sem("x_rows_in")
        dve_chain = sem("dve_chain")
        var_ready = sem("var_ready")
        std_ready = sem("std_ready")
        x_ready = sem("x_ready")
        brow_in = sem("brow_in")
        xplus_ready = sem("xplus_ready")
        u_ready = sem("u_ready")
        nmax_ready = sem("nmax_ready")
        e_ready = sem("e_ready")
        p_ready = sem("p_ready")
        elu_min = sem("elu_min")
        elu_exp = sem("elu_exp")
        elu_rows = sem("elu_rows")
        bias1_in = sem("bias1_in")
        out_done = sem("out_done")

        block = ctx.enter_context(nc.Block())

        def wait_drained(eng, *names):
            most = {}
            for name in names:
                e = "A" if KIND[name] == "A" else "V"
                most[e] = max(most.get(e, 0), DRAINS[name])
            for e, n in most.items():
                eng.wait_ge(drained[e], n)

        def wait_split(eng, n):
            i = (n - 1) // FC
            same = sum((k in BY_POOL) == (i in BY_POOL) for k in range(i))
            eng.wait_ge(low_by_pool if i in BY_POOL else low_by_dve, same * FC + (n - 1) % FC + 1)

        def wait_full(eng, name):
            eng.wait_ge(tile_full, NUMBER[name] + 1)

        def place_hg(queue, m):
            for q in range(B // NM):
                b = m * (B // NM) + q
                for part in range(2):
                    rows = hg[q * NB:(q + 1) * NB, part, m, :].bitcast(F32)
                    queue.dma_start(Mt[(2 + part) * LH:(3 + part) * LH, b, :, :].bitcast(F32),
                                    rows.unsqueeze(1).broadcast_to([NB, 2, F])).then_inc(hg_in[b], 16)

        @block.sync
        def _(sp):
            for k, name in enumerate(("dst", "src", "etype")):
                sp.dma_start(idx[:, k, :], a[name].rearrange("(p c) -> p c", p=P)).then_inc(ints_in, 16)

            loaded = [0]

            def load_until(i, chunk=0):
                while loaded[0] < min(i * FC + chunk, len(WEIGHTS) * FC):
                    j = loaded[0]
                    if j >= RING:
                        sp.wait_ge(chunks_used, j - RING + 1)
                    w = a[WEIGHTS[j // FC]].rearrange("(c p) n -> p c n", p=P)
                    sp.dma_start(raw[:, j % RING, :], w[:, j % FC, :]).then_inc(raw_in[j % RING], 16)
                    loaded[0] += 1

            qT_rows = a["qT"].rearrange("(c p) n -> p c n", p=P)
            sp.dma_start(q_raw[:, :, :], qT_rows).then_inc(q_in, 16)
            load_until(0, 1)
            sp.dma_start(bg_raw[:, :], a["bg"]).then_inc(small_in, 16)
            sp.dma_start(bcol[:, :, :], a["bias_cols"]).then_inc(small_in, 16)
            for k in range(2):
                sp.dma_start(qk[k][:, :, :], a[f"qk{k}"]).then_inc(small_in, 16)
            load_until(1, 1)
            sp.dma_start(x_raw[:, :, :], a["xT"].rearrange("(c p) n -> p c n", p=P)).then_inc(x_in, 16)

            q_rows = a["q"].rearrange("(b h l) f -> b l h f", h=2, l=LH)

            def place_q(g, b, u):
                for n in range(NJ):
                    sp.dma_start(qrep[n * LH:(n + 1) * LH, u, :, :],
                                 q_rows[bass.ds(b, 1), :, :, :].rearrange("o l h f -> (o l) h f")).then_inc(
                        qrep_in[u], 16)

            for g in range(2):
                load_until(GATE_AT[g] - 1, 1)
                wait_drained(sp, ("agg", g, FC - 1))
                for u in range(2):
                    place_q(g, u, u)
                load_until(GATE_AT[g], 1)
                for m in range(NM):
                    wait_drained(sp, ("hg", g, m, 1))
                    place_hg(sp, m)
                load_until(GATE_AT[g] + 1, 1)
                with sp.Fori(1, B // 2) as i2:
                    for u in range(2):
                        sp.wait_ge(prod_ready, i2 * (4 * JS) + (4 + 2 * (STEPS * g + JS * (u - 1))))
                        place_q(g, i2 * 2 + u, u)
            sp.wait_ge(prods_summed, 1 + 2 * REDS)
            sp.dma_start(xrows[:, :, :], a["x"].rearrange("(m p) f -> p m f", p=P)).then_inc(x_rows_in, 16)
            for k in range(2):
                sp.dma_start(brow[:, k, :], a[f"brow{k}"].partition_broadcast(P)).then_inc(brow_in, 16)
            load_until(WEIGHTS.index("gcn3"))
            sp.wait_ge(xplus_ready, 1)
            sp.dma_start(brow[:, 0, :], a["brow2"].partition_broadcast(P)).then_inc(brow_in, 16)
            load_until(WEIGHTS.index("W1_0"), 1)
            sp.wait_ge(xplus_ready, 2)
            sp.dma_start(brow[:, 1, :], a["brow3"].partition_broadcast(P)).then_inc(bias1_in, 16)
            load_until(len(WEIGHTS))
            for m in range(NM):
                for h in range(2):
                    sp.wait_ge(x_ready, 2 * (NM * 3 + m) + h + 1)
                    f = slice(h * FH, (h + 1) * FH)
                    sp.dma_start(result[m * P:(m + 1) * P, f], xrows[:, m, f]).then_inc(out_done, 16)
            sp.wait_ge(out_done, 16 * 2 * NM)

        @block.gpsimd
        def _(pool):
            pool.iota(iota_i[:, :], [[1, F]], base=0, channel_multiplier=0).then_inc(iota_made, 1)
            pool.memset(ident[:, :], 0.0).then_inc(const_made, 1)
            pool.memset(window[:, :], 0.0).then_inc(const_made, 1)
            pool.wait_ge(const_made, 2)
            pool.affine_select(out=ident[:, :], in_=ident[:, :], compare_op=ALU.not_equal, fill=1.0, base=0,
                               pattern=[[-1, P]], channel_multiplier=1).then_inc(const_made, 1)
            for n in range(NJ):
                pool.wait_ge(const_made, 3 + n)
                pool.memset(window[n * LH:(n + 1) * LH, P - NJ + n:P - NJ + n + 1], 1.0).then_inc(const_made, 1)
            pool.wait_ge(const_made, 7)
            pool.memset(ones[:, :].bitcast(F32), 1.0).then_inc(const_made, 1)
            pool.wait_ge(const_made, 8)
            pool.memset(epsc[:, :], EPS).then_inc(const_made, 1)
            pool.wait_ge(q_high, 2)
            for k in range(2):
                c = slice(3 * k, 3 * k + 3)
                pool.tensor_tensor(qT[1][:, c, :], q_raw[:, c, :], qT[0][:, c, :], ALU.subtract).then_inc(q_split, 1)
                pool.wait_ge(q_split, k + 1)
            pool.wait_ge(bg_high, 1)
            pool.tensor_tensor(bg[:, 1, :], bg_raw[:, :], bg[:, 0, :], ALU.subtract).then_inc(bg_split, 1)
            pool.wait_ge(bg_split, 1)

            def split_weight(i):
                for c in range(FC):
                    j = i * FC + c
                    pool.wait_ge(high_made, j + 1)
                    s = j % RING
                    pool.tensor_tensor(Wl[:, s, :], raw[:, s, :], Wh[:, s, :], ALU.subtract).then_inc(
                        low_by_pool, 1)
                    wait_split(pool, j + 1)

            split_weight(BY_POOL[0])
            pool.wait_ge(x_high, 1)
            pool.tensor_tensor(HB[:, 1, :, :], x_raw[:, :, :], HB[:, 0, :, :], ALU.subtract).then_inc(x_split, 1)
            wait_drained(pool, ("qg", 3, 1))
            wait_full(pool, ("AgT", 1))
            pool.wait_ge(x_split, 1)
            for part in range(2):
                for b2 in range(2):
                    for h in range(2):
                        p0 = (2 * b2 + h) * LH
                        dst = Mt[part * LH:(part + 1) * LH, b2:B:2, h, :].bitcast(F32)
                        pool.dma_start(dst, qg[p0:p0 + LH, part, :, :].bitcast(F32)).then_inc(qg_placed, 16)
            pool.sem_inc(halves_added, LAG)
            for g in range(2):
                wait_drained(pool, ("agg", g, FC - 1))
                pool.memset(att[:, ATT - LAG:ATT, 0, :], 0.0).then_inc(att_clean, 1)
                for b in range(B):
                    pool.wait_ge(hg_in[b], 32 * (g + 1))
                    pool.sem_inc(hg_placed, 1)
                with pool.Fori(0, STEPS // ATT) as i:
                    for k in range(ATT):
                        pool.wait_ge(prod_ready, i * (2 * ATT) + (4 + 2 * (STEPS * g + k + 1)))
                        pool.tensor_tensor(att[:, k, 0, :], att[:, k, 0, :], att[:, k, 1, :], ALU.add).then_inc(
                            halves_added, 1)
                pool.wait_ge(tanh_ready, FC * (g + 1))
                pool.tensor_tensor(thT, thT, Hf[:, :, :], ALU.subtract).then_inc(th_ready, 1)
                for c in range(FC):
                    pool.wait_ge(gate_scaled, FC * g + c + 1)
                    pool.tensor_tensor(alpha[:, c, :], alpha[:, c, :], Hf[:, c, :], ALU.add).then_inc(gate_added, 1)
            for k in range(3):
                pool.wait_ge(x_ready, 2 * NM * (k + 1))
                pool.wait_ge(brow_in, 16 * (2 if k < 2 else 3))
                for m in range(NM):
                    ins = pool.tensor_tensor(xplus[:, m, :], xrows[:, m, :], brow[:, k % 2, :], ALU.add)
                ins.then_inc(xplus_ready, 1)
            pool.wait_ge(xplus_ready, 3)
            for i in BY_POOL[1:]:
                split_weight(i)

        @block.tensor
        def _(pe):
            weight = [0]

            def product(out, x, y, start, stop):
                pe.matmul(out, x[0], y[0], start=start, stop=False, skip_group_check=True)
                pe.matmul(out, x[0], y[1], start=False, stop=False, skip_group_check=True)
                return pe.matmul(out, x[1], y[0], start=False, stop=stop, skip_group_check=True)

            def parts(t, *at):
                return [t[(slice(None), part) + at] for part in range(2)]

            def acquire(name):
                i = NUMBER[name]
                if i >= BANKS:
                    wait_drained(pe, TILES[i - BANKS][0])

            def stream(name, groups, operands, ready=None, first=True, last=True):
                i = weight[0]
                assert WEIGHTS[i] == name, (WEIGHTS[i], name)
                weight[0] += 1
                for n, group in enumerate(groups):
                    for c in range(FC):
                        if n == 0:
                            if ready is not None:
                                ready(c)
                            wait_split(pe, FC * i + c + 1)
                        for tile, out in group:
                            if c == 0 and first:
                                acquire(tile)
                            x, y = operands(tile, c, [t[:, (FC * i + c) % RING, :] for t in (Wh, Wl)])
                            mm = product(out, x, y, first and c == 0, last and c == FC - 1)
                            if last and c == FC - 1:
                                mm.then_inc(tile_full, 1)
                        if n == len(groups) - 1 and not (last and c == FC - 1):
                            mm.then_inc(chunks_used, 1)
                if last:
                    pe.drain().then_inc(chunks_used, 1)

            def rows_product(name, tiles, cols, ready=None, first=True, by_rows=False):
                tiles = [(t, psum(t, FH)) for t in tiles]
                groups = [tiles[:2], tiles[2:]] if by_rows else [tiles]
                stream(name, groups,
                       lambda t, c, w: (cols(c, t[-2]), [p[:, t[-1] * FH:(t[-1] + 1) * FH] for p in w]), ready,
                       first)

            def cols_product(name, tiles, x, ready=None, first=True, last=True, by_tile=False):
                tiles = [(t, psum(t, N)) for t in tiles]
                stream(name, [[t] for t in tiles] if by_tile else [tiles],
                       lambda t, c, w: ([p[:, t[-1] * P:(t[-1] + 1) * P] for p in w], parts(x, c)), ready, first, last)

            def of(t):
                return lambda c, m: parts(t, c, slice(m * P, (m + 1) * P))

            def four(*name):
                return [name + (m, h) for m in range(NM) for h in range(2)]

            def six(*name):
                return [name + (c,) for c in range(FC)]

            def after(what):
                return lambda c: pe.wait_ge(cols_out, AFTER[what] + c + 1)

            def qk_rows(k, r):
                C = 2 * HEADS[k]
                i = weight[0]
                assert WEIGHTS[i] == f"W{k + 1}T_{r}"
                weight[0] += 1
                for c in range(FC):
                    wait_split(pe, FC * i + c + 1)
                    for h in range(2):
                        t, f = ("wq", k, r, h), slice(h * FH, (h + 1) * FH)
                        if c == 0:
                            acquire(t)
                        pe.matmul(psum(t, FH, 2 * C), qks[k][:, c, :, :].rearrange("p a c -> p (a c)"),
                                  Wh[:, (FC * i + c) % RING, f], start=(c == 0), stop=False, skip_group_check=True)
                        mm = pe.matmul(psum(t, FH, C), qks[k][:, c, 0, :], Wl[:, (FC * i + c) % RING, f],
                                       start=False, stop=(c == FC - 1), skip_group_check=True)
                        if c == FC - 1:
                            mm.then_inc(tile_full, 1)
                    if c < FC - 1:
                        mm.then_inc(chunks_used, 1)
                pe.drain().then_inc(chunks_used, 1)

            def qk_transposes(k):
                C = 2 * HEADS[k]
                acquire(("wqk", k))
                wait_drained(pe, ("wq", k, R - 1, 0), ("wq", k, R - 1, 1))
                for r in range(R):
                    for c in range(FC):
                        o = c * R * C + r * C
                        mm = pe.matmul(psum(("wqk", k), 512)[:, o:o + C], wq_rows[r][0:2 * C, c * P:(c + 1) * P],
                                       fold[k][:, :], start=True, stop=True)
                mm.then_inc(tile_full, 1)

            def graph_transposes():
                pe.wait_ge(graph_ready, 1)
                for s in range(NM):
                    for r in range(R):
                        acquire(("AnT", s, r))
                        for m in range(NM):
                            mm = pe.transpose(psum(("AnT", s, r), N)[:, m * P:(m + 1) * P],
                                              AnS[:, m, r, s * P:(s + 1) * P], ident[:, :])
                        mm.then_inc(tile_full, 1)
                pe.wait_ge(graph_ready, 2)
                for s in range(NM):
                    acquire(("AgT", s))
                    for m in range(NM):
                        mm = pe.transpose(psum(("AgT", s), N)[:, m * P:(m + 1) * P],
                                          AgS[:, m, s * P:(s + 1) * P], ident[:, :])
                    mm.then_inc(tile_full, 1)

            def edge_chunk(c, u, first, last):
                pe.wait_ge(hot_ready, c + 1)
                for m in range(NM):
                    for h in range(2):
                        mm = pe.matmul(psum(("A", m, h), FH), hot[u][:, F + m * P:F + (m + 1) * P],
                                       hot[u][:, h * FH:(h + 1) * FH], start=first, stop=last,
                                       skip_group_check=True)
                mm.then_inc(hot_used, 1)
                return mm

            pe.sem_inc(prods_summed, 1)
            for u in range(HOT):
                edge_chunk(u, u, u == 0, False)
            with pe.Fori(1, EC // HOT - 1) as i:
                for u in range(HOT):
                    edge_chunk(i * HOT + u, u, False, False)
            for u in range(HOT):
                edge_chunk(EC - HOT + u, u, False, u == HOT - 1)
            pe.drain().then_inc(tile_full, 4)

            pe.wait_ge(q_split, 2)
            pe.wait_ge(const_made, 9)
            pe.wait_ge(bg_split, 1)
            qg_tiles = [("qg", c, h) for c in range(4) for h in range(2)]
            for t in qg_tiles:
                acquire(t)
                for part in range(2):
                    pe.matmul(psum(t, FH), ones[:, :], bg[:, part, t[-1] * FH:(t[-1] + 1) * FH], start=(part == 0),
                              stop=False, skip_group_check=True)
            rows_product("WgT_q", qg_tiles, lambda c, m: [qT[part][:, c, m * P:(m + 1) * P] for part in range(2)],
                         first=False)

            pe.wait_ge(x_split, 1)
            pe.wait_ge(qk_split, 4)
            for g in range(2):
                for r in range(R):
                    if r < R - 1:
                        qk_rows(g, r)
                    if g == 0 and r == 0:
                        graph_transposes()
                    rows_product(f"Wrel{g + 1}_{r}", four("Y", g, r), of(HB),
                                 after("gate0") if g == 1 and r == 0 else None)
                cols_product(f"Wroot{g + 1}", six("agg", g), HB, last=False)
                wait_drained(pe, ("Y", g, R - 1, NM - 1, 1))
                for t in six("agg", g):
                    f = slice(t[-1] * P, (t[-1] + 1) * P)
                    for n in range(R * NM):
                        r, s = n // NM, n % NM
                        mm = product(psum(t, N), parts(Y, s, r, f), parts(AnT, s, r), False, n == R * NM - 1)
                    mm.then_inc(tile_full, 1)
                rows_product("WgT_h", four("hg", g), of(HA), after(f"h{g}"))
                qk_rows(g, R - 1)
                qk_transposes(g)

                def gate_sum(i, k):
                    if k % JS == 0:
                        pe.wait_ge(hg_placed, i * (B // NM) + (B * g + k // JS + 1))
                    for n in range(3):
                        if n < 2:
                            pe.wait_ge(prod_ready, i * STEPS + (2 * (STEPS * g + k) + 1 + n))
                        mm = pe.matmul(gsum[k % 2][:, n * 512:(n + 1) * 512], sel[:, k % JS, :],
                                       Mt_graph[:, bass.ds(i * (B // NM) + k // JS, 1), n * 512:(n + 1) * 512],
                                       start=True, stop=True)
                        if n != 1:
                            mm.then_inc(sum_ready, 1)

                def gate_reduce(k, added):
                    pe.wait_ge(halves_added, added)
                    z = P - NJ - k * NJ
                    for h in range(2):
                        mm = pe.matmul(gqi[h], window[:, z:z + P], att[:, k % ATT, 0, h * FH:(h + 1) * FH],
                                       start=(k == 0), stop=(k == STEPS // NM - 1), skip_group_check=True)
                    mm.then_inc(prods_summed, 1)

                wait_drained(pe, ("wq", g, R - 1, 0), ("wqk", g))
                pe.wait_ge(sel_made, 4)
                pe.wait_ge(att_clean, g + 1)
                if g == 0:
                    pe.wait_ge(qg_placed, 16 * 8)
                with pe.Fori(0, NM) as i:
                    for k in range(STEPS // NM):
                        gate_sum(i, k)
                        if k == LAG:
                            pe.wait_ge(qi_rows, i + (1 + NM * g))
                        gate_reduce((k - LAG) % (STEPS // NM), i * (STEPS // NM) + (STEPS * g + k + 1))
                for k in range(STEPS // NM - LAG, STEPS // NM):
                    gate_reduce(k, STEPS * g + STEPS // NM + k + 1 + LAG)
                pe.wait_ge(qi_rows, 1 + NM * (g + 1))
                for c in range(FC):
                    acquire(("qiT", g, c))
                    for m in range(NM):
                        mm = pe.transpose(psum(("qiT", g, c), N)[:, m * P:(m + 1) * P],
                                          yrows[:, m, c * P:(c + 1) * P], ident[:, :])
                    mm.then_inc(tile_full, 1)

                cols_product("WqT_h", six("alpha", g), HA, last=False)
                cols_product("WqT_q", six("alpha", g), QX, lambda c: wait_drained(pe, ("qiT", g, c)), first=False,
                             by_tile=(g == 1))

            for h in range(2):
                pe.wait_ge(gate_added, FC + (h + 1) * (FC // 2))
                for m in range(NM):
                    acquire(("out", 0, m, h))
                    for c in range(3):
                        mm = pe.transpose(psum(("out", 0, m, h), FH)[:, c * P:(c + 1) * P],
                                          alpha[:, 3 * h + c, m * P:(m + 1) * P], ident[:, :])
                    mm.then_inc(tile_full, 1)

            def to_cols(tiles, rows, ready):
                for m in range(NM):
                    for t in tiles:
                        c = t[-1]
                        if m == 0:
                            acquire(t)
                        if c % (FC // 2) == 0:
                            ready(m, c // (FC // 2))
                        mm = pe.transpose(psum(t, N)[:, m * P:(m + 1) * P], rows[:, m, c * P:(c + 1) * P], ident[:, :])
                        if m == NM - 1:
                            mm.then_inc(tile_full, 1)

            def x_to_cols(k):
                to_cols(six("xT", k), xrows, lambda m, h: pe.wait_ge(x_ready, 2 * (NM * k + m) + h + 1))

            def x_chunk(k):
                return lambda c: wait_drained(pe, ("xT", k, c))

            def gcn_rows(k, n, slot):
                for m in range(NM):
                    for s in range(NM):
                        for h in range(2):
                            t = ("out", k, m, h)
                            if s == 0:
                                acquire(t)
                            if m == 0:
                                wait_drained(pe, ("Yg", n, s, h))
                            mm = product(psum(t, FH), parts(AgT, s, slice(m * P, (m + 1) * P)),
                                         parts(Yg, slot, s, slice(h * FH, (h + 1) * FH)), s == 0, s == NM - 1)
                            if s == NM - 1:
                                mm.then_inc(tile_full, 1)

            x_to_cols(0)
            rows_product("gcn1", four("Yg", 0), of(HB), x_chunk(0), by_rows=True)
            for s in range(NM):
                for t in six("agg", 2):
                    c = t[-1]
                    if s == 0:
                        acquire(t)
                    wait_drained(pe, ("Yg", 0, s, c // (FC // 2)))
                    mm = product(psum(t, N), parts(Yg, 0, s, slice(c * P, (c + 1) * P)), parts(AgT, s),
                                 s == 0, s == NM - 1)
                    if s == NM - 1:
                        mm.then_inc(tile_full, 1)
            rows_product("gcn2", four("Yg", 1), of(HA), after("gcn"), by_rows=True)
            gcn_rows(1, 1, 1)
            x_to_cols(1)
            rows_product("gcn3", four("Yg", 2), of(HB), x_chunk(1), by_rows=True)
            gcn_rows(2, 2, 0)
            x_to_cols(2)

            for k in range(2):
                H, C = HEADS[k], 2 * HEADS[k]
                x = (HB, HA)[k]
                acquire(("KT", k))
                for c in range(FC):
                    wait_drained(pe, ("hT", c) if k else ("xT", 2, c))
                    mm = product(psum(("KT", k), N, R * C), parts(wqk[k], c), parts(x, c), c == 0, c == FC - 1)
                mm.then_inc(tile_full, 1)
                wait_drained(pe, ("KT", k))
                pe.wait_ge(sel_made, 5)
                acquire(("QN", k))
                for m in range(NM):
                    for part in range(2):
                        mm = pe.matmul(psum(("QN", k), 512)[:, m * R * C:(m + 1) * R * C],
                                       KT[0:R * C, part, m * P:(m + 1) * P], ones_at[0:R * C, 0:R * C],
                                       start=(part == 0), stop=(part == 1))
                mm.then_inc(tile_full, 1)
                for i in range((H * R + 1) // 2):
                    acquire(("Kb", k, i))
                    for e in range(2 * i, min(2 * i + 2, H * R)):
                        col = (e % R) * C + H + e // R
                        row = ones_at[0:R * C, col:col + 1].broadcast_to([R * C, P])
                        pe.matmul(psum(("Kb", k, i), 512)[:, (e % 2) * N:(e % 2 + 1) * N],
                                  row, KT[0:R * C, 0, :], start=True, stop=False, skip_group_check=True)
                        mm = pe.matmul(psum(("Kb", k, i), 512)[:, (e % 2) * N:(e % 2 + 1) * N],
                                       row, KT[0:R * C, 1, :], start=False, stop=True, skip_group_check=True)
                    mm.then_inc(tile_full, 1)
                for r in range(R):
                    rows_product(f"W{k + 1}_{r}", four("Yr", k, r), of(x))
                for m in range(NM):
                    for h in range(H):
                        pe.wait_ge(p_ready, k * NM * HEADS[0] + m * H + h + 1)
                        for s in range(NM):
                            name = ("PT", k, m, h, s)
                            acquire(name)
                            for r in range(R):
                                mm = pe.transpose(psum(name, FH)[:, r * P:(r + 1) * P],
                                                  scores[k][:, m, h, r, s * P:(s + 1) * P], ident[:, :])
                            mm.then_inc(tile_full, 1)
                wait_drained(pe, ("PT", k, NM - 1, H - 1, 0), ("PT", k, NM - 1, H - 1, 1),
                             ("Yr", k, R - 1, NM - 1, 1))
                for m in range(NM):
                    for h in range(2):
                        name = ("att", m, h) if k == 0 else ("out", 3, m, h)
                        acquire(name)
                        D = F // H if k == 0 else FH
                        for e in range(FH // D):
                            head = (2 * h + e) if k == 0 else 0
                            f0 = h * FH + e * D
                            out = psum(name, FH)[:, e * D:(e + 1) * D]
                            for n in range(R * NM):
                                r, src, dst = n // NM, n % NM, slice(m * P, (m + 1) * P)
                                first, last = n == 0, n == R * NM - 1
                                if k == 0:
                                    mm = pe.matmul(out, PT[:, src, head, r, dst], Yf[:, src, r, f0:f0 + D],
                                                   start=first, stop=last)
                                else:
                                    mm = product(out, parts(PTs, src, r, dst), parts(Ys, src, r, slice(f0, f0 + D)),
                                                 first, last)
                        mm.then_inc(tile_full, 1)
                if k == 0:
                    to_cols([("hT", c) for c in range(FC)], yrows,
                            lambda m, h: pe.wait_ge(elu_rows, 2 * m + h + 1))

        @block.scalar
        def _(act):
            def drain_copy(name, dst, src):
                wait_full(act, name)
                act.activation(dst, src, ACT.Copy).then_inc(drained["A"], 1)

            split = [0, 0]

            def split_to(i, chunk=0):
                for j in range(split[0], min(i * FC + chunk, len(WEIGHTS) * FC)):
                    act.wait_ge(raw_in[j % RING], 16 * (j // RING + 1))
                    act.activation(Wh[:, j % RING, :], raw[:, j % RING, :], ACT.Copy).then_inc(high_made, 1)
                    split[0] = j + 1

            def split_ahead(chunk=FC - 2):
                split[1] += 1
                split_to(split[1], chunk)

            def warm(function):
                act.activation(scratch[:, :], epsc[:, :], function)

            def split_high(name, dst, src):
                wait_full(act, name)
                act.activation(dst, src, ACT.Copy).then_inc(tile_high, 1)

            def four(*name):
                return [name + (m, h) for m in range(NM) for h in range(2)]

            act.sem_inc(qi_rows, 1)
            act.wait_ge(q_in, 16)
            for k in range(2):
                c = slice(3 * k, 3 * k + 3)
                act.activation(qT[0][:, c, :], q_raw[:, c, :], ACT.Copy).then_inc(q_high, 1)
            act.wait_ge(small_in, 16 * 4)
            act.activation(bg[:, 0, :], bg_raw[:, :], ACT.Copy).then_inc(bg_high, 1)
            split_to(1)
            act.wait_ge(x_in, 16)
            act.activation(HB[:, 0, :, :], x_raw[:, :, :], ACT.Copy).then_inc(x_high, 1)
            for m in range(NM):
                drain_copy(("A", m, 0), Acnt[:, m, :, :].rearrange("p r n -> p (r n)")[:, 0:FH], psum(("A", m, 0), FH))
            act.wait_ge(deg_ready, 1)
            act.activation(cnt[:, :, 7], cnt[:, :, 3], ACT.Sqrt).then_inc(root_ready, 1)
            split_ahead()
            for c in range(4):
                for h in range(2):
                    split_high(("qg", c, h), qg[:, 0, c, h * FH:(h + 1) * FH], psum(("qg", c, h), FH))
            for g in range(2):
                def drain_qk(r):
                    drain_copy(("wq", g, r, 0), wq_rows[r][0:4 * HEADS[g], 0:FH], psum(("wq", g, r, 0), FH, 4 * HEADS[g]))

                for r in range(R):
                    if r < R - 1:
                        split_ahead(2 if (g, r) == (0, 0) else FC - 2)
                        drain_qk(r)
                    if g == 0 and r == 0:
                        for s in range(NM):
                            for k in range(R):
                                split_high(("AnT", s, k), AnT[:, 0, s, k, :], psum(("AnT", s, k), N))
                    split_ahead()
                    if g == 0 and r == 0:
                        act.wait_ge(qg_placed, 16 * 8)
                    for t in four("Y", g, r):
                        split_high(t, Y[:, 0, t[-2], r, t[-1] * FH:(t[-1] + 1) * FH], psum(t, FH))
                if g == 0:
                    act.wait_ge(small_in, 16 * 4)
                split_ahead()
                for c in range(FC):
                    wait_full(act, ("agg", g, c))
                    act.activation(Hf[:, c, :], psum(("agg", g, c), N), ACT.Relu,
                                   bias=bcol[:, g, c:c + 1]).then_inc(drained["A"], 1)
                split_ahead()
                for t in four("hg", g):
                    split_high(t, hg[:, 0, t[-2], t[-1] * FH:(t[-1] + 1) * FH], psum(t, FH))
                split_to(GATE_AT[g])
                warm(ACT.Sigmoid)
                drain_qk(R - 1)
                split_high(("wqk", g), wqk[g][:, 0, :, :].rearrange("p c n -> p (c n)"),
                           psum(("wqk", g), FC * R * 2 * HEADS[g]))

                def sigmoids(first, end):
                    with act.Fori(first // 2, end // 2) as i:
                        for k in range(2):
                            for n in range(2):
                                act.wait_ge(sum_ready, i * 4 + (2 * STEPS * g + 2 * k + n + 1))
                                v = gsum[k][:, CHUNKS[n]]
                                act.activation(v, v, ACT.Sigmoid).then_inc(sig_ready, 1)

                def drain_qi(m):
                    act.wait_ge(prods_summed, 1 + REDS * g + LAG + STEPS // NM * (m + 1))
                    for h in range(2):
                        ins = act.activation(yrows[:, m, h * FH:(h + 1) * FH], gqi[h], ACT.Copy)
                    ins.then_inc(qi_rows, 1)

                half = STEPS // NM + 2
                sigmoids(0, half)
                drain_qi(0)
                sigmoids(half, STEPS)
                drain_qi(1)
                split_to(GATE_AT[g], 2)
                for c in range(FC):
                    wait_full(act, ("qiT", g, c))
                    act.activation(thT[:, c, :], psum(("qiT", g, c), N), ACT.Tanh).then_inc(tanh_ready, 1)
                    split_high(("qiT", g, c), QX[:, 0, c, :], psum(("qiT", g, c), N))
                split_ahead(FC)
                split_ahead(FC)
                if g == 0:
                    split_ahead()
                for c in range(FC):
                    wait_full(act, ("alpha", g, c))
                    act.activation(alpha[:, c, :], psum(("alpha", g, c), N), ACT.Sigmoid,
                                   bias=bcol[:, 2, c:c + 1]).then_inc(drained["A"], 1)

            def layer_norm_std(k):
                warm(ACT.Sqrt)
                for m in range(NM):
                    act.wait_ge(var_ready, NM * k + m + 1)
                    act.activation(mv[:, m, 2:3], mv[:, m, 1:2], ACT.Sqrt, bias=epsc[:, :]).then_inc(std_ready, 1)

            def drain_x(k):
                for c in range(FC):
                    if k == 0:
                        split_to(split[1], c + 1)
                    split_high(("xT", k, c), HB[:, 0, c, :], psum(("xT", k, c), N))

            def drain_gcn(k, slot):
                split_to(split[1] + 1)
                for t in four("Yg", k):
                    if t[-2:] == (1, 0):
                        split_ahead(3)
                    split_high(t, Yg[:, 0, slot, t[-2], t[-1] * FH:(t[-1] + 1) * FH], psum(t, FH))

            act.wait_ge(const_made, 9)
            layer_norm_std(0)
            split_ahead(2)
            drain_x(0)
            drain_gcn(0, 0)
            for c in range(FC):
                wait_full(act, ("agg", 2, c))
                act.activation(Hf[:, c, :], psum(("agg", 2, c), N), ACT.Relu,
                               bias=bcol[:, 3, c:c + 1]).then_inc(drained["A"], 1)
            drain_gcn(1, 1)
            layer_norm_std(1)
            drain_x(1)
            drain_gcn(2, 0)
            layer_norm_std(2)
            drain_x(2)
            for k in range(2):
                H, C = HEADS[k], 2 * HEADS[k]
                split_high(("KT", k), KT[0:R * C, 0, :], psum(("KT", k), N, R * C))
                split_to(split[1] + 1)
                drain_copy(("QN", k), QN[:, :, 0:R * C], psum(("QN", k), NM * R * C).rearrange("p (m c) -> p m c", m=NM))
                wait_drained(act, ("QN", k))
                for i in range((H * R + 1) // 2):
                    wait_full(act, ("Kb", k, i))
                    for e in range(2 * i, min(2 * i + 2, H * R)):
                        h, r = e // R, e % R
                        ins = act.activation(scores[k][:, 0, h, r, :], psum(("Kb", k, i), 512)[:, (e % 2) * N:(e % 2 + 1) * N],
                                             ACT.Identity, bias=QN[:, 0, r * C + h:r * C + h + 1])
                    ins.then_inc(u_ready, 1)
                warm(ACT.Exp)

                def exps(m):
                    act.wait_ge(nmax_ready, NM * k + m + 1)
                    for h in range(H):
                        v = scores[k][:, m, h, :, :].rearrange("p r n -> p (r n)")
                        act.activation(v, v, ACT.Exp, bias=smx[:, m, 1, h:h + 1]).then_inc(e_ready, 1)

                for r in range(R):
                    split_ahead()
                    for m in range(NM):
                        if r == (m if k == 0 else 0):
                            exps(m)
                    for m in range(NM):
                        for h in range(2):
                            t, f = ("Yr", k, r, m, h), slice(h * FH, (h + 1) * FH)
                            if k == 0:
                                drain_copy(t, Yf[:, m, r, f], psum(t, FH))
                            else:
                                split_high(t, Ys[:, 0, m, r, f], psum(t, FH))
                for m in range(NM):
                    for h in range(H):
                        for src in range(NM):
                            t = ("PT", k, m, h, src)
                            v, dst = psum(t, FH).rearrange("p (r n) -> p r n", r=R), slice(m * P, (m + 1) * P)
                            if k == 1:
                                split_high(t, PTs[:, 0, src, :, dst], v)
                            elif src == 0:
                                drain_copy(t, PT[:, 0, h, :, dst], v)
                if k == 0:
                    for m in range(NM):
                        for h in range(2):
                            act.wait_ge(elu_min, 2 * m + h + 1)
                            v = elu_m[:, m, h * FH:(h + 1) * FH]
                            act.activation(v, v, ACT.Exp).then_inc(elu_exp, 1)
                    for c in range(FC):
                        split_high(("hT", c), HA[:, 0, c, :], psum(("hT", c), N))
            layer_norm_std(3)

        @block.vector
        def _(dve):
            links = [0]

            def link(ins):
                links[0] += 1
                ins.then_inc(dve_chain, 1)
                dve.wait_ge(dve_chain, links[0])

            def drain_copy(name, dst, src):
                wait_full(dve, name)
                dve.tensor_copy(dst, src).then_inc(drained["V"], 1)

            split = [0, 0]

            def split_to(i, chunk=0):
                for j in range(split[0], min(i * FC + chunk, len(WEIGHTS) * FC)):
                    if j // FC not in BY_POOL:
                        dve.wait_ge(high_made, j + 1)
                        s = j % RING
                        dve.tensor_tensor(Wl[:, s, :], raw[:, s, :], Wh[:, s, :], ALU.subtract).then_inc(low_by_dve, 1)
                    split[0] = j + 1

            def split_ahead(chunk=FC - 2):
                split[1] += 1
                split_to(split[1], chunk)

            def split_low(name, dst, src, high):
                dve.wait_ge(tile_high, HIGHS[name])
                dve.tensor_tensor(dst, src, high, ALU.subtract).then_inc(drained["V"], 1)

            def four(*name):
                return [name + (m, h) for m in range(NM) for h in range(2)]

            def half(t):
                return slice(t[-1] * FH, (t[-1] + 1) * FH)

            def split_cols(t, c, src):
                link(dve.tensor_copy(t[:, 0, c, :], src))
                dve.tensor_tensor(t[:, 1, c, :], src, t[:, 0, c, :], ALU.subtract).then_inc(cols_out, 1)

            def split_relu(g):
                for c in range(FC):
                    wait_drained(dve, ("agg", g, c))
                    split_cols(HA, c, Hf[:, c, :])

            dve.sem_inc(prod_ready, 4)
            dve.wait_ge(ints_in, 48)
            dve.wait_ge(iota_made, 1)
            dve.tensor_copy(iota_h[:, :], iota_i[:, :])
            link(dve.tensor_copy(idxf[:, :, :], idx[:, :, :]))
            link(dve.scalar_tensor_tensor(out=comb[:, :], in0=idxf[:, 2, :], scalar=float(N), in1=idxf[:, 1, :],
                                          op0=ALU.mult, op1=ALU.add))

            def one_hots(c, u, wait):
                if wait:
                    dve.wait_ge(hot_used, c - (HOT - 1))
                dve.tensor_scalar(hot[u][:, 0:F], iota_h[:, :], comb[:, bass.ds(c, 1)], None, ALU.is_equal)
                dve.tensor_scalar(hot[u][:, F:F + N], iota_h[:, 0:N], idxf[:, 0, bass.ds(c, 1)], None,
                                  ALU.is_equal).then_inc(hot_ready, 1)

            for u in range(HOT):
                one_hots(u, u, False)
            with dve.Fori(1, EC // HOT) as i:
                for u in range(HOT):
                    one_hots(i * HOT + u, u, True)

            dve.wait_ge(const_made, 9)
            v = sel[:, :, :].rearrange("p j (n l) -> p j n l", n=NJ)
            for part in range(2):
                p0 = part * LH
                dve.tensor_copy(v[p0:p0 + LH], ident[p0:p0 + LH, p0:p0 + LH].unsqueeze(1).unsqueeze(1).broadcast_to(
                    [LH, JS, NJ, LH])).then_inc(sel_made, 1)
                p0 = (2 + part) * LH
                dve.tensor_copy(sel[p0:p0 + LH, :, :].rearrange("p j (n l) -> p (j n) l", n=NJ),
                                ident[p0:p0 + LH, p0:p0 + LH].unsqueeze(2).broadcast_to([LH, NB, LH])).then_inc(
                    sel_made, 1)

            for m in range(NM):
                drain_copy(("A", m, 1), Acnt[:, m, :, :].rearrange("p r n -> p (r n)")[:, FH:F], psum(("A", m, 1), FH))
            wait_drained(dve, ("A", 1, 0), ("A", 1, 1))
            link(dve.tensor_reduce(cnt[:, :, 0:R], Acnt[:, :, :, :], AX.X, ALU.add))
            link(dve.tensor_reduce(cnt[:, :, 3:4], cnt[:, :, 0:R], AX.X, ALU.add))
            dve.tensor_scalar(cnt[:, :, 3:4], cnt[:, :, 3:4], 1.0, None, ALU.add).then_inc(deg_ready, 1)
            link(dve.tensor_scalar(cnt[:, :, 4:7], cnt[:, :, 0:R], 1.0, None, ALU.max))
            link(dve.reciprocal(cnt[:, :, 4:7], cnt[:, :, 4:7]))
            for m in range(NM):
                for r in range(R):
                    ins = dve.tensor_scalar(AnS[:, m, r, :], Acnt[:, m, r, :], cnt[:, m, 4 + r:5 + r], None, ALU.mult)
            ins.then_inc(graph_ready, 1)
            link(dve.tensor_tensor(AgS[:, :, :], Acnt[:, :, 0, :], Acnt[:, :, 1, :], ALU.add))
            link(dve.tensor_tensor(AgS[:, :, :], AgS[:, :, :], Acnt[:, :, 2, :], ALU.add))
            for m in range(NM):
                d = AgS[:, m, m * P:(m + 1) * P]
                link(dve.tensor_tensor(d, d, ident[:, :], ALU.add))
            dve.wait_ge(root_ready, 1)
            link(dve.reciprocal(cnt[:, :, 7], cnt[:, :, 7]))
            for m in range(NM):
                ins = dve.tensor_scalar(AgS[:, m, :], AgS[:, m, :], cnt[:, m, 7:8], None, ALU.mult)
            ins.then_inc(graph_ready, 1)

            dve.wait_ge(small_in, 16 * 4)
            for k in range(2):
                C = 2 * HEADS[k]
                link(dve.tensor_copy(qks[k][:, :, 0, :], qk[k][:, :, :]))
                dve.tensor_tensor(qks[k][:, :, 1, :], qk[k][:, :, :], qks[k][:, :, 0, :], ALU.subtract).then_inc(
                    qk_split, 1)
                dve.tensor_tensor(fold[k][:, :], ident[0:2 * C, 0:C], ident[0:2 * C, C:2 * C], ALU.add).then_inc(
                    qk_split, 1)
            split_ahead()
            for c in range(4):
                for h in range(2):
                    f = slice(h * FH, (h + 1) * FH)
                    split_low(("qg", c, h), qg[:, 1, c, f], psum(("qg", c, h), FH), qg[:, 0, c, f])
            for g in range(2):
                def drain_qk(r):
                    drain_copy(("wq", g, r, 1), wq_rows[r][0:4 * HEADS[g], FH:F], psum(("wq", g, r, 1), FH, 4 * HEADS[g]))

                for r in range(R):
                    if r < R - 1:
                        if (g, r) != (1, 0):
                            split_ahead(2 if (g, r) == (0, 0) else FC - 2)
                        drain_qk(r)
                    if g == 0 and r == 0:
                        for s in range(NM):
                            for k in range(R):
                                split_low(("AnT", s, k), AnT[:, 1, s, k, :], psum(("AnT", s, k), N), AnT[:, 0, s, k, :])
                        for s in range(NM):
                            wait_full(dve, ("AgT", s))
                            v = psum(("AgT", s), N)
                            link(dve.tensor_scalar(AgT[:, 0, s, :], v, cnt[:, s, 7:8], None, ALU.mult))
                            dve.scalar_tensor_tensor(out=AgT[:, 1, s, :], in0=v, scalar=cnt[:, s, 7:8], in1=AgT[:, 0, s, :],
                                                     op0=ALU.mult, op1=ALU.subtract).then_inc(drained["V"], 1)
                    split_ahead()
                    for t in four("Y", g, r):
                        split_low(t, Y[:, 1, t[-2], r, half(t)], psum(t, FH), Y[:, 0, t[-2], r, half(t)])
                split_ahead()
                split_relu(g)
                split_ahead()
                for t in four("hg", g):
                    split_low(t, hg[:, 1, t[-2], half(t)], psum(t, FH), hg[:, 0, t[-2], half(t)])
                split_to(GATE_AT[g])
                drain_qk(R - 1)
                v = [wqk[g][:, part, :, :].rearrange("p c n -> p (c n)") for part in range(2)]
                split_low(("wqk", g), v[1], psum(("wqk", g), FC * R * 2 * HEADS[g]), v[0])

                with dve.Fori(0, B // 2) as i2:
                    for k in range(2 * JS):
                        u = k // JS
                        if k % JS == 0:
                            dve.wait_ge(qrep_in[u], i2 * (16 * NJ) + 16 * NJ * (B // 2 * g + 1))
                        dve.wait_ge(prods_summed, i2 * (2 * JS) + (1 + REDS * g + k))
                        for n in range(2):
                            dve.wait_ge(sig_ready, i2 * (4 * JS) + (2 * (STEPS * g + k) + n + 1))
                            dve.tensor_tensor(att_flat[k % ATT][:, CHUNKS[n]], gsum[k % 2][:, CHUNKS[n]],
                                              qrep_flat[u][:, CHUNKS[n]], ALU.mult).then_inc(prod_ready, 1)
                split_to(GATE_AT[g], 2)
                for c in range(FC):
                    split_low(("qiT", g, c), QX[:, 1, c, :], psum(("qiT", g, c), N), QX[:, 0, c, :])
                split_ahead(FC)
                split_ahead(FC)
                if g == 0:
                    split_ahead()
                dve.wait_ge(th_ready, g + 1)
                for c in range(FC):
                    wait_drained(dve, ("alpha", g, c))
                    dve.tensor_tensor(alpha[:, c, :], alpha[:, c, :], thT[:, c, :], ALU.mult).then_inc(gate_scaled, 1)
                if g == 0:
                    for c in range(FC):
                        dve.wait_ge(gate_added, c + 1)
                        split_cols(HB, c, alpha[:, c, :])
                        split_to(split[1] + 1, min(c + 1, FC - 2))
                    split[1] += 1

            def normalise(k, tiles, add):
                def statistics(t):
                    m, h = t[-2:]
                    wait_drained(dve, t)
                    ins = dve.bn_stats(stat[:, m, h, :], y_half(m, h))
                    if h == 1:
                        link(ins)
                        dve.bn_aggr(mv[:, m, 0:2], stat[:, m, :, :]).then_inc(var_ready, 1)

                for n, t in enumerate(tiles):
                    m, h = t[-2:]
                    wait_full(dve, t)
                    add(m, h, psum(t, FH)).then_inc(drained["V"], 1)
                    if n > 0:
                        statistics(tiles[n - 1])
                statistics(tiles[-1])
                for m in range(NM):
                    dve.wait_ge(std_ready, NM * k + m + 1)
                    link(dve.reciprocal(mv[:, m, 3:4], mv[:, m, 2:3]))
                    for h in range(2):
                        f = slice(h * FH, (h + 1) * FH)
                        dve.tensor_scalar(xrows[:, m, f], yrows[:, m, f], mv[:, m, 0:1], mv[:, m, 3:4], ALU.subtract,
                                          ALU.mult).then_inc(x_ready, 1)

            def y_half(m, h):
                return yrows[:, m, h * FH:(h + 1) * FH]

            def drain_x(k):
                for c in range(FC):
                    if k == 0:
                        split_to(split[1], c + 1)
                    split_low(("xT", k, c), HB[:, 1, c, :], psum(("xT", k, c), N), HB[:, 0, c, :])

            def drain_gcn(k, slot):
                split_to(split[1] + 1)
                for t in four("Yg", k):
                    if t[-2:] == (1, 0):
                        split_ahead(3)
                    split_low(t, Yg[:, 1, slot, t[-2], half(t)], psum(t, FH), Yg[:, 0, slot, t[-2], half(t)])

            def residual(k):
                x = xrows if k == 0 else xplus
                normalise(k, [t for t, _ in TILES if t[:2] == ("out", k)], lambda m, h, tile: dve.tensor_tensor(
                    y_half(m, h), tile, x[:, m, h * FH:(h + 1) * FH], ALU.add))

            dve.wait_ge(x_rows_in, 16)
            residual(0)
            split_ahead(0)
            drain_x(0)
            dve.tensor_copy(ones_at, ident[0:R * 2 * HEADS[0], 0:R * 2 * HEADS[0]]).then_inc(sel_made, 1)
            dve.tensor_scalar(hide, Acnt[:, :, :, :], 0.0, -BIG, ALU.is_equal, ALU.mult)
            drain_gcn(0, 0)
            split_relu(2)
            drain_gcn(1, 1)
            dve.wait_ge(xplus_ready, 1)
            residual(1)
            drain_x(1)
            drain_gcn(2, 0)
            dve.wait_ge(xplus_ready, 2)
            residual(2)
            drain_x(2)
            for k in range(2):
                H, C = HEADS[k], 2 * HEADS[k]
                split_low(("KT", k), KT[0:R * C, 1, :], psum(("KT", k), N, R * C), KT[0:R * C, 0, :])
                split_to(split[1] + 1)
                wait_drained(dve, ("QN", k))
                kb = (H * R + 1) // 2
                for i in range(kb):
                    dve.wait_ge(u_ready, k * ((HEADS[0] * R + 1) // 2) + i + 1)
                    for e in range(2 * i, min(2 * i + 2, H * R)):
                        h, r = e // R, e % R
                        ins = dve.tensor_scalar(scores[k][:, 1, h, r, :], psum(("Kb", k, i), 512)[:, (e % 2) * N:(e % 2 + 1) * N],
                                                QN[:, 1, r * C + h:r * C + h + 1], None, ALU.add)
                    ins.then_inc(drained["V"], 1)
                wait_drained(dve, ("Kb", k, kb - 1))
                split_ahead()
                for m in range(NM):
                    v = scores[k][:, m, 0:H, :, :].rearrange("p h r n -> p (h r n)")
                    link(dve.scalar_tensor_tensor(out=v, in0=v, scalar=SLOPE, in1=v, op0=ALU.mult, op1=ALU.max))
                    for h in range(H):
                        v = scores[k][:, m, h, :, :].rearrange("p r n -> p (r n)")
                        ins = dve.tensor_tensor_reduce(v, v, hide[:, m, :, :].rearrange("p r n -> p (r n)"), 1.0,
                                                       -3e38, ALU.add, ALU.max, smx[:, m, 0, h:h + 1])
                    link(ins)
                    dve.tensor_scalar(smx[:, m, 1, 0:H], smx[:, m, 0, 0:H], -1.0, None, ALU.mult).then_inc(nmax_ready, 1)
                for m in range(NM):
                    for h in range(H):
                        dve.wait_ge(e_ready, k * NM * HEADS[0] + m * H + h + 1)
                        v = scores[k][:, m, h, :, :].rearrange("p r n -> p (r n)")
                        ins = dve.tensor_tensor_reduce(v, v, Acnt[:, m, :, :].rearrange("p r n -> p (r n)"), 1.0,
                                                       0.0, ALU.mult, ALU.add, smx[:, m, 2, h:h + 1])
                        ins.then_inc(p_ready, 1)
                    dve.wait_ge(p_ready, k * NM * HEADS[0] + (m + 1) * H)
                    link(dve.tensor_scalar(smx[:, m, 3, 0:H], smx[:, m, 2, 0:H], EPS_Z, None, ALU.add))
                    link(dve.reciprocal(smx[:, m, 3, 0:H], smx[:, m, 3, 0:H]))
                if k == 0:
                    split_ahead()
                    split_ahead()
                else:
                    for r in range(R):
                        if r > 0:
                            split_ahead()
                        for t in four("Yr", k, r):
                            split_low(t, Ys[:, 1, t[-2], r, half(t)], psum(t, FH), Ys[:, 0, t[-2], r, half(t)])
                for m in range(NM):
                    for h in range(H):
                        for src in range(NM):
                            t = ("PT", k, m, h, src)
                            v, dst = psum(t, FH).rearrange("p (r n) -> p r n", r=R), slice(m * P, (m + 1) * P)
                            if k == 1:
                                split_low(t, PTs[:, 1, src, :, dst], v, PTs[:, 0, src, :, dst])
                            elif src == 1:
                                drain_copy(t, PT[:, 1, h, :, dst], v)
                if k == 0:
                    D = F // H
                    dve.wait_ge(bias1_in, 16)
                    for m in range(NM):
                        for h in range(2):
                            wait_full(dve, ("att", m, h))
                            for e in range(2):
                                head = 2 * h + e
                                f = slice(head * D, (head + 1) * D)
                                ins = dve.scalar_tensor_tensor(out=yrows[:, m, f],
                                                               in0=psum(("att", m, h), FH)[:, e * D:(e + 1) * D],
                                                               scalar=smx[:, m, 3, head:head + 1], in1=brow[:, 1, f],
                                                               op0=ALU.mult, op1=ALU.add)
                            ins.then_inc(drained["V"], 1)
                            wait_drained(dve, ("att", m, h))
                            f = slice(h * FH, (h + 1) * FH)
                            t = yrows[:, m, f]
                            dve.tensor_scalar(elu_m[:, m, f], t, 0.0, None, ALU.min).then_inc(elu_min, 1)
                            link(dve.tensor_scalar(t, t, 0.0, -1.0, ALU.max, ALU.add))
                            dve.wait_ge(elu_exp, 2 * m + h + 1)
                            dve.tensor_tensor(t, t, elu_m[:, m, f], ALU.add).then_inc(elu_rows, 1)
                    for c in range(FC):
                        split_low(("hT", c), HA[:, 1, c, :], psum(("hT", c), N), HA[:, 0, c, :])
                else:
                    dve.wait_ge(xplus_ready, 3)
                    normalise(3, four("out", 3), lambda m, h, tile: dve.scalar_tensor_tensor(
                        out=y_half(m, h), in0=tile, scalar=smx[:, m, 3, 0:1], in1=xplus[:, m, h * FH:(h + 1) * FH],
                        op0=ALU.mult, op1=ALU.add))


def kernel(**inputs):
    import numpy as np
    import concourse.bacc as bacc
    from concourse import mybir as mb
    from concourse.bass_utils import run_bass_kernel_spmd as run

    def cols(w):
        return np.ascontiguousarray(np.transpose(w))

    def chunks(v):
        return np.ascontiguousarray(np.swapaxes(v.reshape(FC, P, -1), 0, 1))

    v = {k: np.asarray(x) for k, x in inputs.items()}
    q = v["L0_gnn_query_embs"].reshape(B * L, F)
    arrays = {
        "dst": v["dst"], "src": v["src"], "etype": v["edge_type_3"],
        "x": v["x"], "xT": cols(v["x"]), "q": q, "qT": cols(q), "bg": v["L0_gnn_bg"].reshape(1, F),
        "bias_cols": np.ascontiguousarray(np.stack([v[n].reshape(FC, P).T for n in (
            "L0_gnn_b1", "L0_gnn_b2", "L0_gnn_bq", "L1_gnn_b1")], axis=1)),
        "brow0": v["L1_gnn_b2"], "brow1": v["L2_gnn_b"], "brow2": v["L3_gnn_b2"], "brow3": v["L3_gnn_b1"],
        "qk0": chunks(np.concatenate([v["L3_gnn_q1"], v["L3_gnn_k1"]], axis=1)),
        "qk1": chunks(np.concatenate([v["L3_gnn_q2"], v["L3_gnn_k2"]], axis=1)),
        "WgT_h": cols(v["L0_gnn_Wg"][:, :F]), "WgT_q": cols(v["L0_gnn_Wg"][:, F:]),
        "WqT_h": cols(v["L0_gnn_Wq"][:, :F]), "WqT_q": cols(v["L0_gnn_Wq"][:, F:]),
        "Wroot1": v["L0_gnn_W_root1"], "Wroot2": v["L0_gnn_W_root2"],
        "gcn1": v["L1_gnn_W1"], "gcn2": v["L1_gnn_W2"], "gcn3": v["L2_gnn_W"],
    }
    for r in range(R):
        arrays[f"Wrel1_{r}"] = v["L0_gnn_W_rel1"][r]
        arrays[f"Wrel2_{r}"] = v["L0_gnn_W_rel2"][r]
        arrays[f"W1_{r}"], arrays[f"W1T_{r}"] = v["L3_gnn_W1"][r], cols(v["L3_gnn_W1"][r])
        arrays[f"W2_{r}"], arrays[f"W2T_{r}"] = v["L3_gnn_W2"][r], cols(v["L3_gnn_W2"][r])
    arrays = {k: np.ascontiguousarray(x) for k, x in arrays.items()}
    nc = bacc.Bacc("TRN2", target_bir_lowering=False, num_devices=1)
    a = {k: nc.dram_tensor(f"in_{k}", x.shape, mb.dt.from_np(x.dtype), kind="ExternalInput").ap()
         for k, x in arrays.items()}
    out = nc.dram_tensor("out_x", (N, F), mb.dt.float32, kind="ExternalOutput").ap()
    build(nc, a, out)
    r = run(nc, [{f"in_{k}": x for k, x in arrays.items()}], core_ids=[0])
    return r.results[0]["out_x"]
```
